# Optimizing a Trainium2 kernel written in Bass

```python
import numpy as np
import jax
import jax.numpy as jnp

def _softmax(x, axis=-1):
    return jax.nn.softmax(x, axis=axis)

def _gelu(x):
    return jax.nn.gelu(x, approximate=True)

def _silu(x):
    return jax.nn.silu(x)

def _sigmoid(x):
    return jax.nn.sigmoid(x)

def _layernorm(x, axis=-1, eps=1e-05):
    m = jnp.mean(x, axis=axis, keepdims=True)
    v = jnp.var(x, axis=axis, keepdims=True)
    return (x - m) / jnp.sqrt(v + eps)

def _scatter_add(tgt, idx, src, axis=0):
    return tgt.at[idx].add(src)

def _segment_sum(src, seg, n):
    return jax.ops.segment_sum(src, seg, n)
kernel_name = 'mk_seq_postln_d1_jaxref_r8_c05897'

def setup_inputs(seed: int=0):
    np.random.seed(seed)
    _w = jnp.asarray

    def _L0_attn_setup():
        import jax, jax.numpy as jnp
        import numpy as np
        ROPE_THETA = 10000.0
        N_HEAD = 16

        def _rope(x, theta):
            T, D = (x.shape[-2], x.shape[-1])
            pos = jnp.arange(T, dtype=jnp.float32)
            inv_freq = 1.0 / theta ** (jnp.arange(0, D, 2, dtype=jnp.float32) / D)
            freqs = pos[:, None] * inv_freq[None, :]
            cos = jnp.cos(freqs).astype(x.dtype)[None, None]
            sin = jnp.sin(freqs).astype(x.dtype)[None, None]
            x_even = x[..., ::2]
            x_odd = x[..., 1::2]
            rot = jnp.stack((x_even * cos - x_odd * sin, x_even * sin + x_odd * cos), axis=-1)
            return rot.reshape(x.shape)
        key = jax.random.key(seed)
        ks = jax.random.split(key, 5)
        B, T, E = (4, 256, 128)
        s = 0.02
        return {'x': jax.random.normal(ks[0], (B, T, E), jnp.float32), 'Wqkv': jax.random.normal(ks[1], (E, 3 * E), jnp.float32) * s, 'bqkv': jax.random.normal(ks[2], (3 * E,), jnp.float32) * s, 'Wproj': jax.random.normal(ks[3], (E, E), jnp.float32) * s, 'bproj': jax.random.normal(ks[4], (E,), jnp.float32) * s}
    _L0_attn_in = _L0_attn_setup()

    def _L0_ffn_setup():
        import jax, jax.numpy as jnp
        import numpy as np
        from jax import lax
        DIM = 128
        N_EXPERTS = 16
        TOPK = 4
        N_GROUPS = 4
        TOPK_GROUPS = 2
        ROUTE_SCALE = 1.0
        INTER = 64
        SHARED_INTER = 2 * INTER

        def _gate(x, gate_w):
            T = x.shape[0]
            logits = x @ gate_w.T
            scores = jax.nn.softmax(logits.astype(jnp.float32), axis=-1)
            original_scores = scores
            g = scores.reshape(T, N_GROUPS, N_EXPERTS // N_GROUPS)
            group_scores = g.max(axis=-1)
            _, gidx = lax.top_k(group_scores, TOPK_GROUPS)
            gmask = jnp.zeros_like(group_scores).at[jnp.arange(T)[:, None], gidx].set(1.0)
            masked = (g * gmask[..., None]).reshape(T, N_EXPERTS)
            _, indices = lax.top_k(masked, TOPK)
            weights = jnp.take_along_axis(original_scores, indices, axis=1)
            weights = weights * ROUTE_SCALE
            return (weights.astype(x.dtype), indices)
        key = jax.random.key(seed)
        ks = jax.random.split(key, 8)
        s = lambda fan_in: 1.0 / np.sqrt(fan_in)
        return {'x': jax.random.normal(ks[0], (2, 128, DIM), dtype=jnp.float32), 'gate_w': jax.random.normal(ks[1], (N_EXPERTS, DIM), dtype=jnp.float32) * s(DIM), 'w1': jax.random.normal(ks[2], (N_EXPERTS, DIM, INTER), dtype=jnp.float32) * s(DIM), 'w2': jax.random.normal(ks[3], (N_EXPERTS, INTER, DIM), dtype=jnp.float32) * s(INTER), 'w3': jax.random.normal(ks[4], (N_EXPERTS, DIM, INTER), dtype=jnp.float32) * s(DIM), 'ws1': jax.random.normal(ks[5], (DIM, SHARED_INTER), dtype=jnp.float32) * s(DIM), 'ws2': jax.random.normal(ks[6], (SHARED_INTER, DIM), dtype=jnp.float32) * s(SHARED_INTER), 'ws3': jax.random.normal(ks[7], (DIM, SHARED_INTER), dtype=jnp.float32) * s(DIM)}
    _L0_ffn_in = _L0_ffn_setup()
    _d = {'L0_attn_x': _L0_attn_in['x'], 'L0_attn_Wqkv': _L0_attn_in['Wqkv'], 'L0_attn_bqkv': _L0_attn_in['bqkv'], 'L0_attn_Wproj': _L0_attn_in['Wproj'], 'L0_attn_bproj': _L0_attn_in['bproj'], 'L0_ffn_gate_w': _L0_ffn_in['gate_w'], 'L0_ffn_w1': _L0_ffn_in['w1'], 'L0_ffn_w2': _L0_ffn_in['w2'], 'L0_ffn_w3': _L0_ffn_in['w3'], 'L0_ffn_ws1': _L0_ffn_in['ws1'], 'L0_ffn_ws2': _L0_ffn_in['ws2'], 'L0_ffn_ws3': _L0_ffn_in['ws3']}
    _x0 = _d['L0_attn_x']
    _d['L0_attn_x'] = jax.random.normal(jax.random.fold_in(jax.random.key(seed), 1), (16, 512, 128), dtype=_x0.dtype)
    del _x0
    return _d

def reference(L0_attn_x, L0_attn_Wqkv, L0_attn_bqkv, L0_attn_Wproj, L0_attn_bproj, L0_ffn_gate_w, L0_ffn_w1, L0_ffn_w2, L0_ffn_w3, L0_ffn_ws1, L0_ffn_ws2, L0_ffn_ws3):

    def _L0_attn_ref(x, Wqkv, bqkv, Wproj, bproj):
        import jax, jax.numpy as jnp
        import numpy as np
        ROPE_THETA = 10000.0
        N_HEAD = 16

        def _rope(x, theta):
            T, D = (x.shape[-2], x.shape[-1])
            pos = jnp.arange(T, dtype=jnp.float32)
            inv_freq = 1.0 / theta ** (jnp.arange(0, D, 2, dtype=jnp.float32) / D)
            freqs = pos[:, None] * inv_freq[None, :]
            cos = jnp.cos(freqs).astype(x.dtype)[None, None]
            sin = jnp.sin(freqs).astype(x.dtype)[None, None]
            x_even = x[..., ::2]
            x_odd = x[..., 1::2]
            rot = jnp.stack((x_even * cos - x_odd * sin, x_even * sin + x_odd * cos), axis=-1)
            return rot.reshape(x.shape)
        B, T, E = x.shape
        H = N_HEAD
        D = E // H
        qkv = x @ Wqkv + bqkv
        q, k, v = jnp.split(qkv, 3, axis=-1)
        q = q.reshape(B, T, H, D).transpose(0, 2, 1, 3)
        k = k.reshape(B, T, H, D).transpose(0, 2, 1, 3)
        v = v.reshape(B, T, H, D).transpose(0, 2, 1, 3)
        q = _rope(q, ROPE_THETA)
        k = _rope(k, ROPE_THETA)
        scores = jnp.einsum('bhqd,bhkd->bhqk', q, k) * D ** (-0.5)
        causal = jnp.tril(jnp.ones((T, T), dtype=bool))
        scores = jnp.where(causal[None, None], scores, -jnp.inf)
        weights = jax.nn.softmax(scores, axis=-1)
        out = jnp.einsum('bhqk,bhkd->bhqd', weights, v)
        out = out.transpose(0, 2, 1, 3).reshape(B, T, E)
        return out @ Wproj + bproj

    def _L0_ffn_ref(x, gate_w, w1, w2, w3, ws1, ws2, ws3):
        import jax, jax.numpy as jnp
        import numpy as np
        from jax import lax
        DIM = 128
        N_EXPERTS = 16
        TOPK = 4
        N_GROUPS = 4
        TOPK_GROUPS = 2
        ROUTE_SCALE = 1.0
        INTER = 64
        SHARED_INTER = 2 * INTER

        def _gate(x, gate_w):
            T = x.shape[0]
            logits = x @ gate_w.T
            scores = jax.nn.softmax(logits.astype(jnp.float32), axis=-1)
            original_scores = scores
            g = scores.reshape(T, N_GROUPS, N_EXPERTS // N_GROUPS)
            group_scores = g.max(axis=-1)
            _, gidx = lax.top_k(group_scores, TOPK_GROUPS)
            gmask = jnp.zeros_like(group_scores).at[jnp.arange(T)[:, None], gidx].set(1.0)
            masked = (g * gmask[..., None]).reshape(T, N_EXPERTS)
            _, indices = lax.top_k(masked, TOPK)
            weights = jnp.take_along_axis(original_scores, indices, axis=1)
            weights = weights * ROUTE_SCALE
            return (weights.astype(x.dtype), indices)
        shape = x.shape
        xt = x.reshape(-1, DIM)
        T = xt.shape[0]
        weights, indices = _gate(xt, gate_w)
        c = jnp.zeros((T, N_EXPERTS), dtype=xt.dtype)
        c = c.at[jnp.arange(T)[:, None], indices].add(weights)
        h1 = jnp.einsum('td,edi->tei', xt, w1)
        h3 = jnp.einsum('td,edi->tei', xt, w3)
        a = jax.nn.silu(h1) * h3
        y = jnp.einsum('tei,eid,te->td', a, w2, c)
        z = jax.nn.silu(xt @ ws1) * (xt @ ws3) @ ws2
        return (y + z).reshape(shape)
    x = L0_attn_x
    x = _layernorm(x + _L0_attn_ref(x, L0_attn_Wqkv, L0_attn_bqkv, L0_attn_Wproj, L0_attn_bproj), axis=-1)
    x = _layernorm(x + _L0_ffn_ref(x, L0_ffn_gate_w, L0_ffn_w1, L0_ffn_w2, L0_ffn_w3, L0_ffn_ws1, L0_ffn_ws2, L0_ffn_ws3), axis=-1)
    return x

_drawn_inputs = setup_inputs


def setup_inputs(seed=0):
    import zlib

    import numpy as np

    out = dict(_drawn_inputs(seed))
    spreads = {}
    factors = {'L0_attn_Wqkv': 6.045, 'L0_attn_bqkv': 6.404, 'L0_attn_Wproj': 4.819}
    for name, (base, spread) in spreads.items():
        noise = np.random.default_rng([zlib.crc32(name.encode()), seed]).standard_normal(out[name].shape)
        drawn = base * np.exp(spread * noise) if base else spread * noise
        out[name] = jnp.asarray(drawn.astype(out[name].dtype))
    for name, factor in factors.items():
        out[name] = (out[name] * factor).astype(out[name].dtype)
    return out
```

```python
from contextlib import ExitStack

import numpy as np

import concourse.bass as bass
from concourse import mybir

ALU = mybir.AluOpType
ACT = mybir.ActivationFunctionType
F32 = mybir.dt.float32
BF16 = mybir.dt.bfloat16
I32 = mybir.dt.int32
AX_X = mybir.AxisListType.X

P = 128
B, T, E = 16, 512, 128
H, D = 16, 8
G, HG = 4, 4
TT = T // P
SPLIT = 3
NPROD = SPLIT * SPLIT
KROWS = NPROD * D
KA = 96
MROW = 96
NEXP, INTER = 16, 64
NCH = NEXP * INTER // P
NGRP, EPG = 4, 4
SCALE = float(D) ** -0.5
EPS = 1e-5
MASKED = -3.0e38

SETUP_DVE = 15
SETUP_BIAS = 9
A_UNITS = 11
B_UNITS = 5
A_SPLIT = [(0, 2), (2, 4), (4, 6), (6, 8), (8, 11)]

C_ID, C_COS, C_SIN, C_MASK = 0, P, P + T, P + 2 * T
C_SEL = C_MASK + P
C_L16 = C_SEL + NCH * P
C_L4 = C_L16 + NEXP * NEXP
C_END = C_L4 + NGRP * NGRP


def constants():
    c = np.zeros((P, C_END), np.float32)
    c[:, C_ID:C_ID + P] = np.eye(P, dtype=np.float32)
    inv_freq = (np.float32(1.0) / np.float32(10000.0) ** (np.arange(0, D, 2, dtype=np.float32) / np.float32(D)))
    freqs = np.arange(T, dtype=np.float32)[None, :] * inv_freq.astype(np.float32)[:, None]
    channel_d = (np.arange(P) // HG) % D
    c[:, C_COS:C_COS + T] = np.cos(freqs)[channel_d // 2]
    c[:, C_SIN:C_SIN + T] = np.sin(freqs)[channel_d // 2]
    c[:, C_MASK:C_MASK + P] = np.triu(np.full((P, P), MASKED, np.float32), 1)
    for s in range(SPLIT):
        for e in range(NEXP):
            ch, half = divmod(e, 2)
            at = C_SEL + ch * P + half * INTER
            c[s * NEXP + e, at:at + INTER] = 1.0
    c[:, C_L16:C_L4] = np.tril(np.ones((NEXP, NEXP), np.float32), -1).reshape(1, -1)
    c[:, C_L4:C_END] = np.tril(np.ones((NGRP, NGRP), np.float32), -1).reshape(1, -1)
    return c


ITEMS = [("m1", 0), ("te", -2), ("ta0", -1), ("m2", 0), ("ta1", -1), ("ta2", -1), ("ta3", -1), ("tb", -1),
         ("m3", 0), ("tc", -1), ("v", 1), ("xt", 2), ("q", 2), ("m0", 1), ("qr", 2), ("k", 2), ("kr", 2),
         ("td", -1)]
AT = {(0, 0): "m1", (0, 1): "te", (0, 4): "ta0", (1, 0): "m2", (1, 1): "ta1", (1, 2): "ta2", (1, 3): "ta3",
      (1, 4): "tb", (2, 0): "m3", (2, 1): "tc", (2, 2): "v", (2, 3): "xt", (2, 4): "q", (3, 0): "m0",
      (3, 1): "qr", (3, 2): "k", (3, 3): "kr", (3, 4): "td"}
SHIFT = dict(ITEMS)
ORDER = [n for n, _ in ITEMS]
LOOP = range(3, B - 2)


def exists(b, shift):
    return not isinstance(b, int) or 0 <= b + shift < B


def item_no(b, name):
    if isinstance(b, int):
        before = sum(exists(s, sh) for s in range(-2, b) for _, sh in ITEMS)
        return before + sum(exists(b, SHIFT[n]) for n in ORDER[:ORDER.index(name) + 1])
    return b * len(ITEMS) + (item_no(LOOP[0], name) - LOOP[0] * len(ITEMS))


def wait_alone(engine, semaphore, value):
    if not isinstance(value, int):
        value = engine.to_reg(value)
        engine.wait_ge(semaphore, 1)
    engine.wait_ge(semaphore, value)


class Chain:

    def __init__(self, engine, semaphore):
        self.engine, self.semaphore, self.base, self.n = engine, semaphore, 0, 0

    def __call__(self, instruction):
        instruction.then_inc(self.semaphore, 1)
        self.n += 1

    def wait(self, alone=False):
        if alone:
            wait_alone(self.engine, self.semaphore, self.base + self.n)
        else:
            self.engine.wait_ge(self.semaphore, self.base + self.n)


def run_steps(engine, step, chain=None, first=-2, last=B + 2, loop=LOOP, stride=1):
    for b in range(first, loop[0]):
        step(b)
    if chain is None:
        with engine.Fori(loop[0], loop[-1] + 1) as b:
            step(b)
    else:
        done, chain.n = chain.n, 0
        per = chain.per
        with engine.Fori(loop[0], loop[-1] + 1) as b:
            chain.base = b * per + (done - loop[0] * per)
            step(b)
            assert chain.n == per, (chain.n, per)
        chain.base, chain.n = 0, done + per * len(loop)
    for b in range(loop[-1] + 1, last):
        step(b)


def layer_kernel(nc, x, wqkv, bqkv, wproj, bproj, gate_w, w1, w2, w3, ws1, ws2, ws3, consts, out):
    with ExitStack() as ctx:
        def sb(name, shape, dt=F32):
            return ctx.enter_context(nc.sbuf_tensor(name, shape, dt))

        def dram(name, shape, dt):
            return nc.dram_tensor(name, shape, dt, kind="Internal").ap()

        w = {
            "identf": sb("identf", [P, P]),
            "w1": sb("w1_sb", [P, NEXP, INTER]), "w3": sb("w3_sb", [P, NEXP, INTER]),
            "w2": sb("w2_sb", [P, NCH, E]),
            "ws1": sb("ws1_sb", [P, P]), "ws3": sb("ws3_sb", [P, P]), "ws2": sb("ws2_sb", [P, P]),
            "selb": sb("selb", [SPLIT * NEXP, NCH, P], BF16), "identb": sb("identb", [P, P], BF16),
            "less": sb("less", [P, C_END - C_L16]),
            "x1_d": dram("x1_d", [B, P, TT, E], F32), "x1t_d": dram("x1t_d", [B, P, T], F32),
            "e_d": dram("e_d", [B, P, TT * NEXP], F32),
        }
        attention_pass(nc, w, x, wqkv, bqkv, wproj, bproj, gate_w, w1, w2, w3, ws1, ws2, ws3, consts)
        expert_pass(nc, w, out)


def rsqrt_of(nc, chain, var, y, t, half):
    chain(nc.vector.tensor_scalar(var, var, EPS, None, ALU.add))
    chain.wait()
    chain(nc.vector.tensor_scalar(half.bitcast(I32), var.bitcast(I32), 1, None, ALU.logical_shift_right))
    chain.wait()
    chain(nc.vector.tensor_scalar(y.bitcast(I32), half.bitcast(I32), -1.0, float(0x5F3759DF), ALU.mult, ALU.add))
    chain.wait()
    for _ in range(4):
        chain(nc.vector.tensor_tensor(t, y, y, ALU.mult))
        chain.wait()
        chain(nc.vector.tensor_tensor(t, t, var, ALU.mult))
        chain.wait()
        chain(nc.vector.tensor_scalar(t, t, -0.5, 1.5, ALU.mult, ALU.add))
        chain.wait()
        chain(nc.vector.tensor_tensor(y, y, t, ALU.mult))
        chain.wait()


def layernorm(nc, chain, r, result, st, mv, small, finish):
    for t in range(TT):
        chain(nc.vector.bn_stats(st[:, t, :], r[:, t, :]))
    chain.wait(alone=True)
    for t in range(TT):
        chain(nc.vector.bn_aggr(mv[:, t, :], st[:, t, :]))
    chain.wait()
    chain(nc.vector.tensor_copy(small[:, 3, :], mv[:, :, 1]))
    chain.wait()
    rsqrt_of(nc, chain, small[:, 3, :], small[:, 0, :], small[:, 1, :], small[:, 2, :])
    for t in range(TT):
        last = nc.vector.tensor_scalar(result[:, t, :], r[:, t, :], mv[:, t, 0:1], small[:, 0, t:t + 1],
                                       ALU.subtract, ALU.mult)
        if t < TT - 1:
            chain(last)
    finish(last)


def attention_pass(nc, w, x, wqkv, bqkv, wproj, bproj, gate_w, w1, w2, w3, ws1, ws2, ws3, consts):
    ctx = ExitStack()
    with ctx:
        def sb(name, shape, dt=F32):
            return ctx.enter_context(nc.sbuf_tensor(name, shape, dt))

        def sem(name):
            return ctx.enter_context(nc.semaphore(name))

        identf, identb = w["identf"], w["identb"]
        wraw = sb("wraw", [P, 3 * E])
        wrope = sb("wrope", [P, 4, P])
        brow = sb("brow", [1, 3 * E])
        brope = sb("brope", [1, 4, P])
        bprow = sb("bprow", [1, E])
        ones = sb("ones", [1, P])
        bcol = sb("bcol", [P, 4])
        bv = sb("bv", [P, E])
        bp = sb("bp", [P, E])
        wp = sb("wp", [P, E])
        gwrow = sb("gwrow", [NEXP, E])
        gwt = sb("gwt", [P, NEXP])
        cos = sb("cos", [P, T])
        sin = sb("sin", [P, T])
        maskf = sb("maskf", [P, P])
        maskb = sb("maskb", [P, P], BF16)
        self_ = sb("self_", [SPLIT * NEXP, NCH * P])
        x_in = sb("x_in", [P, TT, E])
        xt = sb("xt", [P, T])
        rope_cos = sb("rope_cos", [P, 2, T])
        rope_sin = sb("rope_sin", [P, 2, T])
        roped = sb("roped", [P, T])
        rest = sb("rest", [P, T])
        parts = sb("parts", [P, 2, SPLIT, T], BF16)
        qs = sb("qs", [P, G, HG * T], BF16)
        ks = sb("ks", [P, G, HG * T], BF16)
        vstage = sb("vstage", [P, TT, E])
        v = sb("v", [P, G, TT, HG, 32])
        mx = sb("mx", [P, G, HG, TT])
        negm = sb("negm", [P, SPLIT, HG * TT], BF16)
        mrest = sb("mrest", [P, 2, HG * TT])
        mrows = sb("mrows", [SPLIT * HG * TT, P], BF16)
        probs = sb("probs", [P, 2, B_UNITS, 2 * T])
        ot = sb("ot", [P, G, T])
        rden = sb("rden", [P, H])
        o = sb("o", [P, TT, E])
        ot2 = sb("ot2", [P, T])
        xres = sb("xres", [P, TT, E])
        xb = sb("xb", [P, TT, E])
        r = sb("r", [P, TT, E])
        st = sb("st", [P, TT, 6])
        mv = sb("mv", [P, TT, 2])
        small = sb("small", [P, 4, TT])
        x1 = sb("x1", [P, TT, E])
        x1t = sb("x1t", [P, T])
        lmax = sb("lmax", [P, TT])
        z = sb("z", [P, TT, NEXP])
        ez = sb("ez", [P, TT * NEXP])

        bounce = nc.dram_tensor("bounce", [B, 2, NPROD, P, T], BF16, kind="Internal").ap()

        psA = [ctx.enter_context(nc.psum_tensor(f"psA{i}", [P, T], F32)) for i in range(2)]
        psB = [ctx.enter_context(nc.psum_tensor(f"psB{i}", [P, 2 * T], F32)) for i in range(2)]
        psO = ctx.enter_context(nc.psum_tensor("psO", [P, T], F32))
        psM = ctx.enter_context(nc.psum_tensor("psM", [P, T], F32))

        consts_in = sem("consts_in")
        setup_dve = sem("setup_dve")
        setup_pe = sem("setup_pe")
        setup_pool = sem("setup_pool")
        x_in_loaded = sem("x_in_loaded")
        xres_loaded = sem("xres_loaded")
        parts_ready = sem("parts_ready")
        bounced = sem("bounced")
        qk_loaded = [sem(f"qk_loaded{g}") for g in range(G)]
        mrows_loaded = [sem(f"mrows_loaded{g}") for g in range(G)]
        a_scored = sem("a_scored")
        a_reduced = sem("a_reduced")
        negm_ready = sem("negm_ready")
        b_scored = sem("b_scored")
        exp_done = sem("exp_done")
        causal_done = sem("causal_done")
        pv_done = sem("pv_done")
        ot_copied = sem("ot_copied")
        v_copied = sem("v_copied")
        item_full = sem("item_full")
        item_free = sem("item_free")
        xb_ready = sem("xb_ready")
        x1_ready = sem("x1_ready")
        ez_ready = sem("ez_ready")
        x1_stored = sem("x1_stored")
        x1t_stored = sem("x1t_stored")
        ez_stored = sem("ez_stored")
        dve_own = sem("dve_own")
        pool_own = sem("pool_own")

        xv = x.rearrange("b (t p) e -> b p t e", p=P)

        block = ctx.enter_context(nc.Block())

        @block.sync
        def _(sp):
            for dst, src in (
                (identf[:, :], consts[:, C_ID:C_ID + P]), (wraw[:, :], wqkv), (brow[:, :], bqkv.rearrange("(a n) -> a n", a=1)),
                (bprow[:, :], bproj.rearrange("(a n) -> a n", a=1)), (cos[:, :], consts[:, C_COS:C_COS + T]),
                (sin[:, :], consts[:, C_SIN:C_SIN + T]), (maskf[:, :], consts[:, C_MASK:C_MASK + P]),
                (gwrow[:, :], gate_w), (wp[:, :], wproj), (self_[:, :], consts[0:SPLIT * NEXP, C_SEL:C_L16]),
                (w["less"][:, :], consts[:, C_L16:C_END]), (w["w1"][:, :, :], w1.rearrange("e d i -> d e i")),
                (w["w3"][:, :, :], w3.rearrange("e d i -> d e i")),
                (w["w2"][:, :, :], w2.rearrange("e i d -> (e i) d").rearrange("(c p) d -> p c d", p=P)),
                (w["ws1"][:, :], ws1), (w["ws3"][:, :], ws3), (w["ws2"][:, :], ws2),
            ):
                sp.dma_start(dst, src).then_inc(consts_in, 16)

            def load_group(b, g):
                wait_alone(sp, bounced, 96 * (b + 1))
                if exists(b, -1):
                    wait_alone(sp, b_scored, 20 * b - 20 + 5 * g + 5)
                for side, dst in ((0, qs), (1, ks)):
                    sp.dma_start(dst[0:KROWS, g, :],
                                 bounce[b, side][:, 32 * g:32 * g + 32, :].rearrange("a (d h) t -> a d (h t)", h=HG)
                                 ).then_inc(qk_loaded[g], 16)

            def load_mrows(b, g, body, item):
                wait_alone(sp, item_free, item_no(body, item))
                sp.dma_start(qs[MROW:MROW + SPLIT, g, :], mrows[:, :]).then_inc(mrows_loaded[g], 16)

            def step(b):
                if exists(b, 0):
                    load_group(b, 3)
                if exists(b, 2):
                    if exists(b, 1):
                        wait_alone(sp, item_full, item_no(b - 1, "xt"))
                    sp.dma_start(x_in[:, :, :], xv[b + 2]).then_inc(x_in_loaded, 16)
                if exists(b, 0):
                    load_mrows(b, 1, b, "m1")
                if exists(b, 1):
                    for side in range(2):
                        wait_alone(sp, parts_ready, 2 * (b + 1) + side + 1)
                        for n in range(SPLIT):
                            rows = bounce[b + 1, 0][n::SPLIT] if side == 0 else bounce[b + 1, 1][SPLIT * n:SPLIT * n + SPLIT]
                            sp.dma_start(rows.rearrange("i p t -> p i t"), parts[:, side, :, :]).then_inc(bounced, 16)
                if exists(b, -1):
                    if exists(b, -2):
                        wait_alone(sp, xb_ready, b - 1)
                    sp.dma_start(xres[:, :, :], xv[b - 1]).then_inc(xres_loaded, 16)
                if exists(b, -2):
                    wait_alone(sp, x1_ready, b - 1)
                    sp.dma_start(w["x1_d"][b - 2], x1[:, :, :]).then_inc(x1_stored, 16)
                    wait_alone(sp, item_free, item_no(b - 1, "td"))
                    sp.dma_start(w["x1t_d"][b - 2], x1t[:, :]).then_inc(x1t_stored, 16)
                if exists(b, 1):
                    load_group(b + 1, 0)
                if exists(b, 0):
                    load_mrows(b, 2, b, "m2")
                if exists(b, -2):
                    wait_alone(sp, ez_ready, b - 1)
                    sp.dma_start(w["e_d"][b - 2], ez[:, :]).then_inc(ez_stored, 16)
                if exists(b, 1):
                    load_group(b + 1, 1)
                if exists(b, 0):
                    load_mrows(b, 3, b, "m3")
                if exists(b, 1):
                    load_group(b + 1, 2)
                    load_mrows(b + 1, 0, b, "m0")

            run_steps(sp, step)
            sp.wait_ge(x1_stored, 16 * B)
            sp.wait_ge(x1t_stored, 16 * B)
            sp.wait_ge(ez_stored, 16 * B)

        @block.gpsimd
        def _(pool):
            chain = Chain(pool, pool_own)
            chain.per = 8
            nc.gpsimd.memset(qs[:, :, :], 0.0).then_inc(setup_pool, 1)
            nc.gpsimd.memset(ks[:, :, :], 0.0).then_inc(setup_pool, 1)
            nc.gpsimd.memset(v[:, :, :, :, :], 0.0).then_inc(setup_pool, 1)
            pool.wait_ge(setup_pool, 3)
            nc.gpsimd.memset(ks[MROW:MROW + SPLIT, :, :], 1.0).then_inc(setup_pool, 1)
            pool.wait_ge(setup_pool, 4)
            nc.gpsimd.memset(v[:, :, :, :, D:D + 1], 1.0).then_inc(setup_pool, 1)
            pool.wait_ge(setup_pool, 5)

            def copy_v(b, g, body_of_v):
                wait_alone(pool, item_free, item_no(body_of_v, "v"))
                if exists(b, -1):
                    wait_alone(pool, pv_done, 4 * b - 4 + g + 1)
                nc.gpsimd.tensor_copy(v[:, g, :, :, 0:D],
                                      vstage[:, :, 32 * g:32 * g + 32].rearrange("p t (h d) -> p t h d", d=D)
                                      ).then_inc(v_copied, 1)

            def split_start(body, batch, side):
                pool.wait_ge(item_free, item_no(body, "qr" if side == 0 else "kr"))
                if exists(batch, -1):
                    pool.wait_ge(bounced, 96 * batch)
                chain(nc.gpsimd.tensor_tensor(roped[:, :], rope_cos[:, side, :], rope_sin[:, side, :], ALU.add))
                chain.wait(alone=True)
                chain(nc.gpsimd.tensor_copy(parts[:, side, 0, :], roped[:, :]))
                chain.wait()

            def split_end(side):
                chain(nc.gpsimd.tensor_tensor(rest[:, :], roped[:, :], parts[:, side, 0, :], ALU.subtract))
                chain.wait(alone=True)
                chain(nc.gpsimd.tensor_copy(parts[:, side, 1, :], rest[:, :]))
                chain.wait()
                nc.gpsimd.tensor_tensor(parts[:, side, 2, :], rest[:, :], parts[:, side, 1, :],
                                        ALU.subtract).then_inc(parts_ready, 1)

            def causal(ap, heads):
                return nc.gpsimd.affine_select(out=ap, in_=ap, compare_op=ALU.is_ge, fill=0.0, base=0,
                                               pattern=[[0, heads], [1, P]], channel_multiplier=-1)

            def step(b):
                for t in range(G):
                    for u in range(B_UNITS):
                        if exists(b, 0):
                            wait_alone(pool, exp_done, 20 * b + 5 * t + u + 1)
                            unit = probs[:, t % 2, u, :]
                            if u < HG:
                                causal(unit.rearrange("p (a n) -> p a n", n=T)[:, :, 0:P], 2)
                                causal(unit[:, T + 384:2 * T].rearrange("p (a n) -> p a n", a=1), 1).then_inc(causal_done, 1)
                            else:
                                causal(unit.rearrange("p (a n) -> p a n", a=HG)[:, :, 0:P], HG).then_inc(causal_done, 1)
                        if (t, u) == (0, 0) and exists(b, 1):
                            split_end(1)
                        if (t, u) == (1, 0) and exists(b, 0):
                            copy_v(b, 3, b - 1)
                        if (t, u) == (1, 1) and exists(b, -1):
                            pool.wait_ge(xres_loaded, 16 * b)
                            if exists(b, -2):
                                pool.wait_ge(item_free, item_no(b - 1, "tc"))
                            nc.gpsimd.tensor_tensor(xb[:, :, :], xres[:, :, :],
                                                    bp[:, :].rearrange("p (a n) -> p a n", a=1).broadcast_to([P, TT, E]),
                                                    ALU.add).then_inc(xb_ready, 1)
                        if (t, u) == (3, 2) and exists(b, 2):
                            split_start(b, b + 2, 0)
                        if (t, u) == (3, 3) and exists(b, 2):
                            split_end(0)
                        if (t, u) == (3, 4):
                            if exists(b, 1):
                                for g in range(3):
                                    copy_v(b + 1, g, b)
                            if exists(b, 2):
                                split_start(b, b + 2, 1)

            pool.wait_ge(setup_dve, SETUP_DVE)
            run_steps(pool, step, chain)

        @block.scalar
        def _(act):
            def step(b):
                for t in range(G):
                    for u in range(B_UNITS):
                        if exists(b, 0):
                            n = 20 * b + 5 * t + u
                            act.wait_ge(b_scored, n + 1)
                            if t >= 2:
                                act.wait_ge(pv_done, 4 * b + t - 1)
                            elif exists(b, -1):
                                act.wait_ge(pv_done, 4 * b + t - 1)
                            nc.scalar.activation(probs[:, t % 2, u, :], psB[(5 * t + u) % 2][:, :], ACT.Exp,
                                                 scale=SCALE).then_inc(exp_done, 1)
                        if u == 3 and exists(b, 0 if t else -1):
                            act.wait_ge(pv_done, 4 * b + t)
                            if t == 1 and exists(b, -1):
                                act.wait_ge(item_full, item_no(b, "ta3"))
                            nc.scalar.copy(ot[:, (t - 1) % G, :], psO[:, :]).then_inc(ot_copied, 1)
                        if (t, u) == (0, 3) and exists(b, -2):
                            act.wait_ge(item_free, item_no(b, "te"))
                            if exists(b, -3):
                                act.wait_ge(ez_stored, 16 * (b - 2))
                            nc.scalar.activation(ez[:, :], z[:, :, :].rearrange("p t e -> p (t e)"), ACT.Exp).then_inc(ez_ready, 1)
                        item = AT.get((t, u))
                        if item in ("tb", "xt", "td") and exists(b, SHIFT[item]):
                            act.wait_ge(item_full, item_no(b, item))
                            if item == "td" and exists(b, -2):
                                act.wait_ge(x1t_stored, 16 * (b - 1))
                            dst = {"tb": ot2, "xt": xt, "td": x1t}[item]
                            nc.scalar.copy(dst[:, :], psM[:, :]).then_inc(item_free, 1)

            run_steps(act, step)

        @block.tensor
        def _(pe):
            pe.wait_ge(setup_dve, SETUP_BIAS)
            for i in range(4):
                nc.tensor.matmul(psM[:, i:i + 1], brope[0:1, i, :], ones[0:1, 0:1], start=True, stop=True)
            nc.tensor.matmul(psM[:, 8:8 + E], ones[0:1, :], brow[0:1, 2 * E:3 * E], start=True, stop=True)
            nc.tensor.matmul(psM[:, 136:136 + E], ones[0:1, :], bprow[0:1, :], start=True, stop=True)
            nc.tensor.transpose(psM[:, 264:264 + NEXP], gwrow[:, :], identf[0:NEXP, 0:NEXP]).then_inc(setup_pe, 1)
            pe.wait_ge(setup_dve, SETUP_DVE)
            pe.wait_ge(setup_pool, 5)

            def item(b, name):
                no = item_no(b, name)
                if not (isinstance(no, int) and no == 1):
                    wait_alone(pe, item_free, no - 1)
                if name in ("m0", "m1", "m2", "m3"):
                    g = int(name[1])
                    wait_alone(pe, negm_ready, 4 * (b + (g == 0)) + g + 1)
                    last = nc.tensor.transpose(psM[:, :].bitcast(BF16)[0:SPLIT * HG * TT, 0:P],
                                               negm[:, :, :].rearrange("p s n -> p (s n)"), identb[:, :])
                elif name == "xt":
                    pe.wait_ge(x_in_loaded, 16 * (b + 3))
                    for t in range(TT):
                        last = nc.tensor.transpose(psM[:, P * t:P * t + P], x_in[:, t, :], identf[:, :])
                elif name == "v":
                    for t in range(TT):
                        last = nc.tensor.matmul(psM[:, P * t:P * t + P], xt[:, P * t:P * t + P], wraw[:, 2 * E:3 * E],
                                                start=True, stop=True)
                elif name in ("q", "qr", "k", "kr"):
                    last = nc.tensor.matmul(psM[:, :], wrope[:, ("q", "qr", "k", "kr").index(name), :], xt[:, :],
                                            start=True, stop=True)
                elif name[:2] == "ta":
                    t = int(name[2])
                    pe.wait_ge(ot_copied, 4 * b)
                    for g in range(G):
                        last = nc.tensor.transpose(psM[:, P * g:P * g + P], ot[:, g, P * t:P * t + P], identf[:, :])
                elif name == "tb":
                    for t in range(TT):
                        last = nc.tensor.transpose(psM[:, P * t:P * t + P], o[:, t, :], identf[:, :])
                elif name == "tc":
                    for t in range(TT):
                        last = nc.tensor.matmul(psM[:, P * t:P * t + P], ot2[:, P * t:P * t + P], wp[:, :],
                                                start=True, stop=True)
                elif name == "td":
                    pe.wait_ge(x1_ready, b)
                    for t in range(TT):
                        last = nc.tensor.transpose(psM[:, P * t:P * t + P], x1[:, t, :], identf[:, :])
                elif name == "te":
                    for t in range(TT):
                        last = nc.tensor.matmul(psM[:, NEXP * t:NEXP * t + NEXP], x1t[:, P * t:P * t + P], gwt[:, :],
                                                start=True, stop=True)
                last.then_inc(item_full, 1)

            def score_a(b, g, unit):
                if unit < 8:
                    qt, heads = (3, [unit]) if unit < 4 else (2, [unit - 4])
                else:
                    qt, heads = (1, [2 * unit - 16, 2 * unit - 15]) if unit < 10 else (0, range(HG))
                if unit == 0:
                    pe.wait_ge(qk_loaded[g], 32 * (b + 1))
                n = 44 * b + 11 * g + unit
                if not (isinstance(n, int) and n < 2):
                    pe.wait_ge(a_reduced, n - 1)
                bank, width = psA[(11 * g + unit) % 2], P * (qt + 1)
                for i, h in enumerate(heads):
                    nc.tensor.matmul(bank[:, width * i:width * i + width],
                                     qs[0:KA, g, T * h + P * qt:T * h + P * qt + P], ks[0:KA, g, T * h:T * h + width],
                                     start=True, stop=False)
                    last = nc.tensor.matmul(bank[:, width * i + width - P:width * i + width], identb[:, :], maskb[:, :],
                                            start=False, stop=True)
                last.then_inc(a_scored, 1)

            def score_b(b, g, u):
                n = 20 * b + 5 * g + u
                if u == 0:
                    pe.wait_ge(mrows_loaded[g], 16 * (b + 1))
                if not (isinstance(n, int) and n < 2):
                    pe.wait_ge(exp_done, n - 1)
                dst = psB[(5 * g + u) % 2]
                if u < HG:
                    todo = [(T * u, 0, 0), (T * u, 1, T), (T * u, 3, T + 384)]
                else:
                    todo = [(T * h, 2, 256 * h) for h in range(HG)]
                for at, kt, col in todo:
                    last = nc.tensor.matmul(dst[:, col:col + T - P * kt], ks[:, g, at + P * kt:at + P * kt + P],
                                            qs[:, g, at + P * kt:at + T], start=True, stop=True)
                last.then_inc(b_scored, 1)

            def weigh(b, g, part):
                kt = (0, 1, 3, 2)[part]
                if part == 0:
                    if not (isinstance(b, int) and 4 * b + g < 1):
                        pe.wait_ge(ot_copied, 4 * b + g)
                    pe.wait_ge(v_copied, 4 * b + g + 1)
                for h in range(HG):
                    if part == 0:
                        pe.wait_ge(causal_done, 20 * b + 5 * g + h + 1)
                    if part == 3 and h == 0:
                        pe.wait_ge(causal_done, 20 * b + 5 * g + 5)
                    unit, at = (h, (0, T, 0, T + 384)[kt]) if kt != 2 else (HG, 256 * h)
                    last = nc.tensor.matmul(psO[32 * h:32 * h + 32, P * kt:T], v[:, g, kt, h, :],
                                            probs[:, g % 2, unit, at:at + T - P * kt],
                                            start=(part == 0), stop=(part == 3))
                if part == 3:
                    last.then_inc(pv_done, 1)

            def step(b):
                for t in range(G):
                    for u in range(B_UNITS):
                        if exists(b, 0):
                            score_b(b, t, u)
                        ahead, ga = (0, t + 2) if t < 2 else (1, t - 2)
                        if exists(b, ahead):
                            for unit in range(*A_SPLIT[u]):
                                score_a(b + ahead, ga, unit)
                        back, gp = (0, t - 1) if t else (-1, 3)
                        if u < 4 and exists(b, back):
                            weigh(b + back, gp, u)
                        name = AT.get((t, u))
                        if name and exists(b, SHIFT[name]):
                            item(b, name)

            run_steps(pe, step)

        @block.vector
        def _(dve):
            chain = Chain(dve, dve_own)
            chain.per = 48
            dve.wait_ge(consts_in, 16 * 17)
            nc.vector.tensor_copy(identb[:, :], identf[:, :]).then_inc(setup_dve, 1)
            nc.vector.memset(ones[:, :], 1.0).then_inc(setup_dve, 1)

            def spread(dst, src):
                plain = dst[:, 0, :].rearrange("p (g d h) -> p g h d", g=G, d=D)
                turned = dst[:, 1, :].rearrange("p (g d two h) -> p g h d two", g=G, d=D // 2, two=2)
                given = src.rearrange("p (g h d) -> p g h d", g=G, h=HG)
                pairs = src.rearrange("p (g h d two) -> p g h d two", g=G, h=HG, two=2)
                for g in range(G):
                    nc.vector.tensor_copy(plain[:, g], given[:, g])
                    nc.vector.tensor_scalar(turned[:, g, :, :, 0], pairs[:, g, :, :, 1], -1.0, None, ALU.mult)
                    last = nc.vector.tensor_copy(turned[:, g, :, :, 1], pairs[:, g, :, :, 0])
                last.then_inc(setup_dve, 1)

            for side in range(2):
                spread(wrope[:, 2 * side:2 * side + 2, :], wraw[:, E * side:E * side + E])
                spread(brope[:, 2 * side:2 * side + 2, :], brow[:, E * side:E * side + E])
            nc.vector.tensor_copy(maskb[:, :], maskf[:, :]).then_inc(setup_dve, 1)
            nc.vector.tensor_copy(w["selb"][:, :, :].rearrange("p c n -> p (c n)"), self_[:, :]).then_inc(setup_dve, 1)
            nc.vector.memset(st[:, :, :], 0.0).then_inc(setup_dve, 1)
            dve.wait_ge(setup_pe, 1)
            nc.vector.tensor_copy(bcol[:, :], psM[:, 0:4]).then_inc(setup_dve, 1)
            nc.vector.tensor_copy(bv[:, :], psM[:, 8:8 + E]).then_inc(setup_dve, 1)
            nc.vector.tensor_copy(bp[:, :], psM[:, 136:136 + E]).then_inc(setup_dve, 1)
            nc.vector.tensor_copy(gwt[:, :], psM[:, 264:264 + NEXP]).then_inc(setup_dve, 1)
            nc.vector.memset(small[:, :, :], 0.0).then_inc(setup_dve, 1)
            nc.vector.memset(mv[:, :, :], 0.0).then_inc(setup_dve, 1)
            dve.wait_ge(setup_dve, SETUP_DVE)

            def reduce_a(b, g, unit):
                dve.wait_ge(a_scored, 44 * b + 11 * g + unit + 1)
                bank = psA[(11 * g + unit) % 2]
                if unit < 8:
                    qt, h0, n = (3, unit, 1) if unit < 4 else (2, unit - 4, 1)
                else:
                    qt, h0, n = (1, 2 * unit - 16, 2) if unit < 10 else (0, 0, HG)
                width = P * (qt + 1)
                nc.vector.tensor_reduce(mx[:, g, h0:h0 + n, qt],
                                        bank[:, 0:width * n].rearrange("p (a n) -> p a n", a=n),
                                        AX_X, ALU.max).then_inc(a_reduced, 1)

            def split_max(b, g):
                dve.wait_ge(a_reduced, 44 * b + 11 * g + 11)
                m = mx[:, g, :, :].rearrange("p h t -> p (h t)")
                chain(nc.vector.tensor_scalar(negm[:, 0, :], m, -1.0, None, ALU.mult))
                chain.wait()
                chain(nc.vector.scalar_tensor_tensor(out=mrest[:, 0, :], in0=m, scalar=-1.0, in1=negm[:, 0, :],
                                                     op0=ALU.mult, op1=ALU.subtract))
                chain.wait()
                chain(nc.vector.tensor_copy(negm[:, 1, :], mrest[:, 0, :]))
                chain.wait()
                nc.vector.tensor_tensor(negm[:, 2, :], mrest[:, 0, :], negm[:, 1, :], ALU.subtract).then_inc(negm_ready, 1)

            def item(b, name):
                dve.wait_ge(item_full, item_no(b, name))
                if name in ("m0", "m1", "m2", "m3"):
                    g = int(name[1])
                    if g:
                        dve.wait_ge(mrows_loaded[g - 1], 16 * (b + 1))
                    elif exists(b, 0):
                        dve.wait_ge(mrows_loaded[3], 16 * (b + 1))
                    nc.vector.tensor_copy(mrows[:, :], psM[:, :].bitcast(BF16)[0:SPLIT * HG * TT, 0:P]).then_inc(item_free, 1)
                elif name == "v":
                    if exists(b, 0):
                        dve.wait_ge(v_copied, 4 * b + 4)
                    nc.vector.tensor_tensor(vstage[:, :, :], psM[:, :].rearrange("p (t e) -> p t e", t=TT),
                                            bv[:, :].rearrange("p (a n) -> p a n", a=1).broadcast_to([P, TT, E]),
                                            ALU.add).then_inc(item_free, 1)
                elif name in ("q", "qr", "k", "kr"):
                    side, turned = name[0] == "k", len(name) == 2
                    if not turned and exists(b, 1):
                        dve.wait_ge(parts_ready, 2 * (b + 2) - 1 + side)
                    dst, table = (rope_sin, sin) if turned else (rope_cos, cos)
                    nc.vector.scalar_tensor_tensor(out=dst[:, int(side), :], in0=psM[:, :],
                                                   scalar=bcol[:, 2 * side + turned:2 * side + turned + 1],
                                                   in1=table[:, :], op0=ALU.add, op1=ALU.mult).then_inc(item_free, 1)
                elif name[:2] == "ta":
                    t = int(name[2])
                    got = psM[:, :].rearrange("p (h c) -> p h c", h=H)
                    chain(nc.vector.reciprocal(rden[:, :], got[:, :, D]))
                    chain.wait()
                    nc.vector.tensor_tensor(o[:, t, :].rearrange("p (h d) -> p h d", h=H), got[:, :, 0:D],
                                            rden[:, :].rearrange("p (h a) -> p h a", a=1).broadcast_to([P, H, D]),
                                            ALU.mult).then_inc(item_free, 1)
                elif name == "tc":
                    dve.wait_ge(xb_ready, b)
                    nc.vector.tensor_tensor(r[:, :, :], psM[:, :].rearrange("p (t e) -> p t e", t=TT), xb[:, :, :],
                                            ALU.add).then_inc(item_free, 1)
                    dve.wait_ge(item_free, item_no(b, name))
                    if exists(b, -2):
                        dve.wait_ge(x1_stored, 16 * (b - 1))
                    layernorm(nc, chain, r, x1, st, mv, small, lambda last: last.then_inc(x1_ready, 1))
                elif name == "te":
                    logits = psM[:, 0:TT * NEXP].rearrange("p (t e) -> p t e", t=TT)
                    chain(nc.vector.tensor_reduce(lmax[:, :], logits, AX_X, ALU.max))
                    chain.wait()
                    if exists(b, -3):
                        dve.wait_ge(ez_ready, b - 2)
                    nc.vector.tensor_tensor(z[:, :, :], logits,
                                            lmax[:, :].rearrange("p (t a) -> p t a", a=1).broadcast_to([P, TT, NEXP]),
                                            ALU.subtract).then_inc(item_free, 1)

            def step(b):
                for t in range(G):
                    for u in range(B_UNITS):
                        ahead, gm = (0, t + 1) if t < 3 else (1, 0)
                        if u == 0 and exists(b, ahead):
                            split_max(b + ahead, gm)
                        ahead, ga = (0, t + 2) if t < 2 else (1, t - 2)
                        if exists(b, ahead):
                            for unit in range(*A_SPLIT[u]):
                                reduce_a(b + ahead, ga, unit)
                        name = AT.get((t, u))
                        if name and name not in ("tb", "xt", "td") and exists(b, SHIFT[name]):
                            item(b, name)

            run_steps(dve, step, chain)


def expert_pass(nc, w, out):
    NC1 = NCH + 1
    ctx = ExitStack()
    with ctx:
        def sb(name, shape, dt=F32):
            return ctx.enter_context(nc.sbuf_tensor(name, shape, dt))

        def sem(name):
            return ctx.enter_context(nc.semaphore(name))

        identf, identb = w["identf"], w["identb"]
        less16 = w["less"][:, 0:NEXP * NEXP].rearrange("p (e f) -> p e f", e=NEXP)
        less4 = w["less"][:, NEXP * NEXP:].rearrange("p (e f) -> p e f", e=NGRP)
        w1f = w["w1"][:, :, :].rearrange("p e i -> p (e i)")
        w3f = w["w3"][:, :, :].rearrange("p e i -> p (e i)")
        w2f = w["w2"][:, :, :].rearrange("p c d -> p (c d)")

        x1 = [sb(f"x1_{i}", [P, TT, E]) for i in range(2)]
        x1t = [sb(f"x1t_{i}", [P, T]) for i in range(2)]
        ez = sb("ez2", [P, TT, NEXP])
        ct = [sb(f"ct_{i}", [SPLIT * NEXP, T], BF16) for i in range(2)]
        esum = sb("esum", [P, TT])
        erec = sb("erec", [P, TT])
        score = sb("score", [P, TT, NEXP])
        gmax = sb("gmax", [P, TT, NGRP])
        gd = sb("gd", [P, TT, NGRP, NGRP])
        ge = sb("ge", [P, TT, NGRP, NGRP])
        grank = sb("grank", [P, TT, NGRP])
        masked = sb("masked", [P, TT, NEXP])
        ed = sb("ed", [P, TT, NEXP, NEXP])
        ee = sb("ee", [P, TT, NEXP, NEXP])
        erank = sb("erank", [P, TT, NEXP])
        c = sb("c", [P, TT, NEXP])
        crest = sb("crest", [P, TT, NEXP])
        cparts = sb("cparts", [P, TT, SPLIT, NEXP], BF16)
        s = [sb(f"s_{i}", [P, T]) for i in range(2)]
        sh = [sb(f"sh_{i}", [P, T]) for i in range(2)]
        a = [sb(f"a_{i}", [P, T]) for i in range(2)]
        yt = sb("yt", [P, T])
        r = sb("r2", [P, TT, E])
        st = sb("st2", [P, TT, 6])
        mv = sb("mv2", [P, TT, 2])
        small = sb("small2", [P, 4, TT])
        res = sb("res", [P, TT, E])

        psH1 = [ctx.enter_context(nc.psum_tensor(f"psH1_{i}", [P, T], F32)) for i in range(2)]
        psH3 = [ctx.enter_context(nc.psum_tensor(f"psH3_{i}", [P, T], F32)) for i in range(2)]
        psC = [ctx.enter_context(nc.psum_tensor(f"psC_{i}", [P, T], F32)) for i in range(2)]
        psY = ctx.enter_context(nc.psum_tensor("psY", [P, T], F32))
        psM = ctx.enter_context(nc.psum_tensor("psM2", [P, T], F32))

        x1_loaded = [sem(f"x1_loaded{i}") for i in range(2)]
        x1t_loaded = [sem(f"x1t_loaded{i}") for i in range(2)]
        ez_loaded = sem("ez_loaded")
        cparts_ready = sem("cparts_ready")
        ct_transposed = sem("ct_transposed")
        ct_copied = sem("ct_copied")
        h1_ready = sem("h1_ready")
        hc_ready = sem("hc_ready")
        silu_ready = sem("silu_ready")
        act_ready = sem("act_ready")
        y_added = sem("y_added")
        yt_copied = sem("yt_copied")
        y_turned = sem("y_turned")
        y_taken = sem("y_taken")
        res_ready = sem("res_ready")
        out_stored = sem("out_stored")
        own = sem("dve_own2")

        ov = out.rearrange("b (t p) e -> b p t e", p=P)
        block = ctx.enter_context(nc.Block())

        def run_pairs(engine, step, chain=None):
            step(0, 0)
            step(1, 1)
            if chain is not None:
                done, chain.n = chain.n, 0
            with engine.Fori(1, B // 2 - 1) as i:
                for par in range(2):
                    if chain is not None and par == 0:
                        chain.base = i * (2 * chain.per) + (done - 2 * chain.per)
                    step(i * 2 + par, par)
            if chain is not None:
                assert chain.n == 2 * chain.per, chain.n
                chain.base, chain.n = 0, done + 2 * chain.per * (B // 2 - 2)
            step(B - 2, 0)
            step(B - 1, 1)

        def first(b):
            return isinstance(b, int) and b == 0

        def last_batch(b):
            return isinstance(b, int) and b == B - 1

        @block.sync
        def _(sp):
            def load(b, par):
                if not first(b):
                    wait_alone(sp, cparts_ready, b)
                sp.dma_start(ez[:, :, :], w["e_d"][b].rearrange("p (t e) -> p t e", t=TT)).then_inc(ez_loaded, 16)
                if not (isinstance(b, int) and b < 2):
                    wait_alone(sp, hc_ready, NC1 * (b - 1))
                sp.dma_start(x1t[par][:, :], w["x1t_d"][b]).then_inc(x1t_loaded[par], 16)
                if not (isinstance(b, int) and b < 2):
                    wait_alone(sp, y_taken, b - 1)
                sp.dma_start(x1[par][:, :, :], w["x1_d"][b]).then_inc(x1_loaded[par], 16)

            def step(b, par):
                if not last_batch(b):
                    load(b + 1, 1 - par)
                if not first(b):
                    wait_alone(sp, res_ready, b)
                    sp.dma_start(ov[b - 1], res[:, :, :]).then_inc(out_stored, 16)

            load(0, 0)
            run_pairs(sp, step)
            wait_alone(sp, res_ready, B)
            sp.dma_start(ov[B - 1], res[:, :, :]).then_inc(out_stored, 16)
            wait_alone(sp, out_stored, 16 * B)

        @block.scalar
        def _(act):
            def copy_ct(b, par):
                act.wait_ge(ct_transposed, b + 1)
                nc.scalar.copy(ct[par][:, :], psM[:, :].bitcast(BF16)[0:SPLIT * NEXP, 0:T]).then_inc(ct_copied, 1)

            def copy_y(b):
                act.wait_ge(y_added, NC1 * b + NC1)
                nc.scalar.copy(yt[:, :], psY[:, :]).then_inc(yt_copied, 1)

            def step(b, par):
                for ch in range(NC1):
                    n, bank = NC1 * b + ch, (par * NC1 + ch) % 2
                    act.wait_ge(h1_ready, n + 1)
                    if not (isinstance(n, int) and n < 2):
                        act.wait_ge(act_ready, n - 1)
                    nc.scalar.activation(s[bank][:, :], psH1[bank][:, :], ACT.Silu).then_inc(silu_ready, 1)
                    if ch == 0 and not first(b):
                        copy_y(b - 1)
                    if ch == 5 and not last_batch(b):
                        copy_ct(b + 1, 1 - par)

            copy_ct(0, 0)
            run_pairs(act, step)
            copy_y(B - 1)

        @block.tensor
        def _(pe):
            def turn_c(b, par):
                wait_alone(pe, cparts_ready, b + 1)
                if not first(b):
                    pe.wait_ge(ct_copied, b)
                if not (isinstance(b, int) and b < 2):
                    pe.wait_ge(y_taken, b - 1)
                for t in range(TT):
                    last = nc.tensor.transpose(psM[:, :].bitcast(BF16)[0:SPLIT * NEXP, P * t:P * t + P],
                                               cparts[:, t, :, :].rearrange("p s e -> p (s e)"), identb[:, :])
                last.then_inc(ct_transposed, 1)

            def turn_y(b):
                pe.wait_ge(yt_copied, b + 1)
                pe.wait_ge(ct_copied, b + 2 if not (isinstance(b, int) and b + 2 > B) else B)
                for t in range(TT):
                    last = nc.tensor.transpose(psM[:, P * t:P * t + P], yt[:, P * t:P * t + P], identf[:, :])
                last.then_inc(y_turned, 1)

            def hidden(b, par, ch):
                n, bank = NC1 * b + ch, (par * NC1 + ch) % 2
                wa, wb = (w1f[:, P * ch:P * ch + P], w3f[:, P * ch:P * ch + P]) if ch < NCH else (w["ws1"][:, :], w["ws3"][:, :])
                if not (isinstance(n, int) and n < 2):
                    pe.wait_ge(act_ready, n - 1)
                nc.tensor.matmul(psH1[bank][:, :], wa, x1t[par][:, :], start=True, stop=True).then_inc(h1_ready, 1)
                last = nc.tensor.matmul(psH3[bank][:, :], wb, x1t[par][:, :], start=True, stop=True)
                if ch < NCH:
                    last = nc.tensor.matmul(psC[bank][:, :], w["selb"][:, ch, :], ct[par][:, :], start=True, stop=True)
                last.then_inc(hc_ready, 1)

            def down(b, par, ch):
                n = NC1 * b + ch
                pe.wait_ge(act_ready, n + 1)
                if ch == 0 and not first(b):
                    pe.wait_ge(yt_copied, b)
                wc = w2f[:, E * ch:E * ch + E] if ch < NCH else w["ws2"][:, :]
                nc.tensor.matmul(psY[:, :], wc, a[(par * NC1 + ch) % 2][:, :], start=(ch == 0),
                                 stop=(ch == NCH)).then_inc(y_added, 1)

            def step(b, par):
                pe.wait_ge(x1t_loaded[par], (b - par) * 8 + 16)
                pe.wait_ge(ct_copied, b + 1)
                for ch in range(NC1):
                    hidden(b, par, ch)
                    if ch:
                        down(b, par, ch - 1)
                    elif not first(b):
                        down(b - 1, 1 - par, NCH)
                    if ch == 2 and not first(b):
                        turn_y(b - 1)
                    if ch == 5 and not last_batch(b):
                        turn_c(b + 1, 1 - par)

            turn_c(0, 0)
            run_pairs(pe, step)
            down(B - 1, 1, NCH)
            turn_y(B - 1)

        @block.vector
        def _(dve):
            chain = Chain(dve, own)
            chain.per = 16 + 9 + 31

            def bcast(ap, shape):
                return ap.broadcast_to(shape)

            def router_groups(b):
                dve.wait_ge(ez_loaded, 16 * (b + 1))
                chain(nc.vector.tensor_reduce(esum[:, :], ez[:, :, :], AX_X, ALU.add))
                chain.wait()
                chain(nc.vector.reciprocal(erec[:, :], esum[:, :]))
                chain.wait()
                chain(nc.vector.tensor_tensor(score[:, :, :], ez[:, :, :],
                                              bcast(erec[:, :].rearrange("p (t a) -> p t a", a=1), [P, TT, NEXP]), ALU.mult))
                chain.wait()
                chain(nc.vector.tensor_reduce(gmax[:, :, :].rearrange("p t g -> p (t g)"),
                                              score[:, :, :].rearrange("p t (g e) -> p (t g) e", g=NGRP), AX_X, ALU.max))
                chain.wait()
                rank(gmax, gd, ge, grank, less4, NGRP)
                chain(nc.vector.scalar_tensor_tensor(
                    out=masked[:, :, :].rearrange("p t (g e) -> p (t g) e", g=NGRP),
                    in0=bcast(grank[:, :, :].rearrange("p t (g a) -> p (t g) a", a=1), [P, TT * NGRP, EPG]),
                    scalar=1.5, in1=score[:, :, :].rearrange("p t (g e) -> p (t g) e", g=NGRP),
                    op0=ALU.is_lt, op1=ALU.mult))
                chain.wait()

            def rank(values, diff, before, result, less, n):
                chain(nc.vector.tensor_tensor(
                    diff[:, :, :, :], bcast(values[:, :, :].rearrange("p t (a f) -> p t a f", a=1), [P, TT, n, n]),
                    bcast(values[:, :, :].rearrange("p t (e a) -> p t e a", a=1), [P, TT, n, n]), ALU.subtract))
                chain.wait()
                chain(nc.vector.scalar_tensor_tensor(
                    out=before[:, :, :, :], in0=diff[:, :, :, :], scalar=0.0,
                    in1=bcast(less.rearrange("p (a e) f -> p a e f", a=1), [P, TT, n, n]), op0=ALU.is_equal, op1=ALU.mult))
                chain.wait()
                chain(nc.vector.scalar_tensor_tensor(
                    out=before[:, :, :, :], in0=diff[:, :, :, :], scalar=0.0, in1=before[:, :, :, :],
                    op0=ALU.is_gt, op1=ALU.add))
                chain.wait()
                chain(nc.vector.tensor_reduce(result[:, :, :], before[:, :, :, :], AX_X, ALU.add))
                chain.wait()

            def router_experts(b):
                rank(masked, ed, ee, erank, less16, NEXP)
                chain(nc.vector.scalar_tensor_tensor(out=c[:, :, :], in0=erank[:, :, :], scalar=3.5, in1=score[:, :, :],
                                                     op0=ALU.is_lt, op1=ALU.mult))
                chain.wait()
                if not first(b):
                    dve.wait_ge(ct_transposed, b)
                chain(nc.vector.tensor_copy(cparts[:, :, 0, :], c[:, :, :]))
                chain.wait()
                chain(nc.vector.tensor_tensor(crest[:, :, :], c[:, :, :], cparts[:, :, 0, :], ALU.subtract))
                chain.wait()
                chain(nc.vector.tensor_copy(cparts[:, :, 1, :], crest[:, :, :]))
                chain.wait()
                nc.vector.tensor_tensor(cparts[:, :, 2, :], crest[:, :, :], cparts[:, :, 1, :],
                                        ALU.subtract).then_inc(cparts_ready, 1)

            def finish(b, par):
                dve.wait_ge(y_turned, b + 1)
                dve.wait_ge(x1_loaded[par], (b - par) * 8 + 16)
                nc.vector.tensor_tensor(r[:, :, :], psM[:, :].rearrange("p (t e) -> p t e", t=TT), x1[par][:, :, :],
                                        ALU.add).then_inc(y_taken, 1)
                dve.wait_ge(y_taken, b + 1)
                if not first(b):
                    dve.wait_ge(out_stored, 16 * b)
                layernorm(nc, chain, r, res, st, mv, small, lambda last: last.then_inc(res_ready, 1))

            def step(b, par):
                for ch in range(NC1):
                    n, bank = NC1 * b + ch, (par * NC1 + ch) % 2
                    dve.wait_ge(silu_ready, n + 1)
                    dve.wait_ge(hc_ready, n + 1)
                    if not (isinstance(n, int) and n < 2):
                        dve.wait_ge(y_added, n - 1)
                    if ch < NCH:
                        chain(nc.vector.tensor_tensor(sh[bank][:, :], s[bank][:, :], psH3[bank][:, :], ALU.mult))
                        chain.wait()
                        nc.vector.tensor_tensor(a[bank][:, :], sh[bank][:, :], psC[bank][:, :], ALU.mult).then_inc(act_ready, 1)
                    else:
                        nc.vector.tensor_tensor(a[bank][:, :], s[bank][:, :], psH3[bank][:, :], ALU.mult).then_inc(act_ready, 1)
                    if ch == 1 and not last_batch(b):
                        router_groups(b + 1)
                    if ch == 2 and not first(b):
                        finish(b - 1, 1 - par)
                    if ch == 3 and not last_batch(b):
                        router_experts(b + 1)

            router_groups(0)
            router_experts(0)
            run_pairs(dve, step, chain)
            finish(B - 1, 1)


_INS = ["L0_attn_x", "L0_attn_Wqkv", "L0_attn_bqkv", "L0_attn_Wproj", "L0_attn_bproj", "L0_ffn_gate_w",
        "L0_ffn_w1", "L0_ffn_w2", "L0_ffn_w3", "L0_ffn_ws1", "L0_ffn_ws2", "L0_ffn_ws3"]
_OUTS = [((B, T, E), "float32")]


def kernel(**inputs):
    import concourse.bacc as _bacc
    from concourse.bass_utils import run_bass_kernel_spmd as _run

    nc = _bacc.Bacc("TRN2", target_bir_lowering=False, num_devices=1)
    arrays, args = {}, []
    for name in _INS:
        arrays[f"in_{name}"] = np.ascontiguousarray(inputs[name])
    arrays["in_constants"] = constants()
    for name, a in arrays.items():
        args.append(nc.dram_tensor(name, a.shape, mybir.dt.from_np(a.dtype), kind="ExternalInput").ap())
    for i, (shape, dtype) in enumerate(_OUTS):
        args.append(nc.dram_tensor(f"out_{i}", shape, mybir.dt.from_np(np.dtype(dtype)), kind="ExternalOutput").ap())
    layer_kernel(nc, *args)
    r = _run(nc, [arrays], core_ids=[0])
    return r.results[0]["out_0"]
```

```python
from contextlib import ExitStack

import numpy as np

import concourse.bass as bass
from concourse import mybir

ALU = mybir.AluOpType
ACT = mybir.ActivationFunctionType
F32 = mybir.dt.float32
F32R = mybir.dt.float32r
BF16 = mybir.dt.bfloat16
I32 = mybir.dt.int32
AX_X = mybir.AxisListType.X

P = 128
B, T, E = 16, 512, 128
H, D = 16, 8
G, HG = 4, 4
TT = T // P
SPLIT = 3
NPROD = SPLIT * SPLIT
KROWS = NPROD * D
KA = 96
MROW = 96
NEXP, INTER = 16, 64
NCH = NEXP * INTER // P
NGRP, EPG = 4, 4
TOP_GROUPS, TOP_EXPERTS = 2, 4
SCALE = float(D) ** -0.5
EPS = 1e-5
MASKED = -3.0e38

SETUP_DVE = 14
SETUP_BIAS = 8
A_UNITS = 11
B_UNITS = 5
A_SPLIT = [(0, 2), (2, 4), (4, 6), (6, 8), (8, 11)]

C_ID, C_COS, C_SIN, C_MASK = 0, P, P + T, P + 2 * T
C_SEL = C_MASK + P
C_L16 = C_SEL + NCH * P
C_L4 = C_L16 + NEXP * NEXP
C_END = C_L4 + NGRP * NGRP


def constants():
    c = np.zeros((P, C_END), np.float32)
    c[:, C_ID:C_ID + P] = np.eye(P, dtype=np.float32)
    inv_freq = (np.float32(1.0) / np.float32(10000.0) ** (np.arange(0, D, 2, dtype=np.float32) / np.float32(D)))
    freqs = np.arange(T, dtype=np.float32)[None, :] * inv_freq.astype(np.float32)[:, None]
    channel_d = (np.arange(P) // HG) % D
    c[:, C_COS:C_COS + T] = np.cos(freqs)[channel_d // 2]
    c[:, C_SIN:C_SIN + T] = np.sin(freqs)[channel_d // 2]
    c[:, C_MASK:C_MASK + P] = np.triu(np.full((P, P), MASKED, np.float32), 1)
    for s in range(SPLIT):
        for e in range(NEXP):
            ch, half = divmod(e, 2)
            at = C_SEL + ch * P + half * INTER
            c[s * NEXP + e, at:at + INTER] = 1.0
    c[:, C_L16:C_L4] = np.tril(np.ones((NEXP, NEXP), np.float32), -1).reshape(1, -1)
    c[:, C_L4:C_END] = np.tril(np.ones((NGRP, NGRP), np.float32), -1).reshape(1, -1)
    return c


ITEMS = [("m1", 0), ("xt", 2), ("q", 2), ("qr", 2), ("ta3", -1), ("m2", 0), ("k", 2), ("kr", 2), ("tb", -1),
         ("ta0", 0), ("m3", 0), ("tc", -1), ("v", 2), ("ta1", 0), ("m0", 1), ("td", -1), ("te", -1), ("ta2", 0)]
AT = {(0, 0): "m1", (0, 1): "xt", (0, 2): "q", (0, 3): "qr", (0, 4): "ta3", (1, 0): "m2", (1, 1): "k",
      (1, 2): "kr", (1, 3): "tb", (1, 4): "ta0", (2, 0): "m3", (2, 1): "tc", (2, 2): "v", (2, 4): "ta1",
      (3, 0): "m0", (3, 2): "td", (3, 3): "te", (3, 4): "ta2"}
SHIFT = dict(ITEMS)
ORDER = [n for n, _ in ITEMS]
LOOP = range(3, B - 3)


def exists(b, shift):
    return not isinstance(b, int) or 0 <= b + shift < B


def item_no(b, name):
    if isinstance(b, int):
        before = sum(exists(s, sh) for s in range(-2, b) for _, sh in ITEMS)
        return before + sum(exists(b, SHIFT[n]) for n in ORDER[:ORDER.index(name) + 1])
    return b * len(ITEMS) + (item_no(LOOP[0], name) - LOOP[0] * len(ITEMS))


def wait_alone(engine, semaphore, value):
    if not isinstance(value, int):
        value = engine.to_reg(value)
        engine.wait_ge(semaphore, 1)
    engine.wait_ge(semaphore, value)


class Chain:

    def __init__(self, engine, semaphore):
        self.engine, self.semaphore, self.base, self.n = engine, semaphore, 0, 0

    def __call__(self, instruction):
        instruction.then_inc(self.semaphore, 1)
        self.n += 1

    def wait(self, alone=False):
        if alone:
            wait_alone(self.engine, self.semaphore, self.base + self.n)
        else:
            self.engine.wait_ge(self.semaphore, self.base + self.n)


def run_steps(engine, step, chain=None, first=-2, last=B + 1, loop=LOOP, stride=1):
    for b in range(first, loop[0]):
        step(b)
    if chain is None:
        with engine.Fori(loop[0], loop[-1] + 1) as b:
            step(b)
    else:
        done, chain.n = chain.n, 0
        per = chain.per
        with engine.Fori(loop[0], loop[-1] + 1) as b:
            chain.base = b * per + (done - loop[0] * per)
            step(b)
            assert chain.n == per, (chain.n, per)
        chain.base, chain.n = 0, done + per * len(loop)
    for b in range(loop[-1] + 1, last):
        step(b)


def layer_kernel(nc, x, wqkv, bqkv, wproj, bproj, gate_w, w1, w2, w3, ws1, ws2, ws3, consts, out):
    with ExitStack() as ctx:
        def sb(name, shape, dt=F32):
            return ctx.enter_context(nc.sbuf_tensor(name, shape, dt))

        def dram(name, shape, dt):
            return nc.dram_tensor(name, shape, dt, kind="Internal").ap()

        w = {
            "identf": sb("identf", [P, P]),
            "w1h": sb("w1h", [P, (NCH + 1) * P], F32R), "w1l": sb("w1l", [P, (NCH + 1) * P], F32R),
            "w3h": sb("w3h", [P, (NCH + 1) * P], F32R), "w3l": sb("w3l", [P, (NCH + 1) * P], F32R),
            "w2h": sb("w2h", [P, (NCH + 1) * P], F32R), "w2l": sb("w2l", [P, (NCH + 1) * P], F32R),
            "selb": sb("selb", [SPLIT * NEXP, NCH, P], BF16), "identb": sb("identb", [P, P], BF16),
            "less": sb("less", [P, C_END - C_L16]),
            "x1_d": dram("x1_d", [B, P, TT, E], F32), "x1t_d": dram("x1t_d", [B, P, T], F32),
            "e_d": dram("e_d", [B, P, TT * NEXP], F32),
        }
        attention_pass(nc, w, x, wqkv, bqkv, wproj, bproj, gate_w, w1, w2, w3, ws1, ws2, ws3, consts)
        expert_pass(nc, w, out)


def norm_moments(nc, chain, r, st, mv):
    for t in range(TT):
        chain(nc.vector.bn_stats(st[:, t, :], r[:, t, :]))
    chain.wait(alone=True)
    for t in range(TT):
        chain(nc.vector.bn_aggr(mv[:, t, :], st[:, t, :]))
    chain.wait()


def norm_rsqrt(nc, chain, mv, small):
    y, t, var, half = (small[:, n, :] for n in range(4))
    chain(nc.vector.tensor_scalar(var, mv[:, :, 1], EPS, None, ALU.add))
    chain.wait()
    chain(nc.vector.tensor_scalar(t.bitcast(I32), var.bitcast(I32), 1, None, ALU.logical_shift_right))
    chain(nc.vector.tensor_scalar(half, var, -0.5, None, ALU.mult))
    chain.wait()
    chain(nc.vector.tensor_scalar(y.bitcast(I32), t.bitcast(I32), -1.0, float(0x5F3759DF), ALU.mult, ALU.add))
    chain.wait()
    for _ in range(3):
        chain(nc.vector.tensor_tensor(t, y, y, ALU.mult))
        chain.wait()
        chain(nc.vector.tensor_tensor(t, t, half, ALU.mult))
        chain.wait()
        chain(nc.vector.scalar_tensor_tensor(out=y, in0=t, scalar=1.5, in1=y, op0=ALU.add, op1=ALU.mult))
        chain.wait()


def norm_apply(nc, chain, r, result, mv, small, done):
    for t in range(TT):
        last = nc.vector.tensor_scalar(result[:, t, :], r[:, t, :], mv[:, t, 0:1], small[:, 0, t:t + 1],
                                       ALU.subtract, ALU.mult)
        if t < TT - 1:
            chain(last)
    last.then_inc(done, 1)


NORM_CHAIN = 2 * TT + 4 + 9 + TT - 1


def attention_pass(nc, w, x, wqkv, bqkv, wproj, bproj, gate_w, w1, w2, w3, ws1, ws2, ws3, consts):
    ctx = ExitStack()
    with ctx:
        def sb(name, shape, dt=F32):
            return ctx.enter_context(nc.sbuf_tensor(name, shape, dt))

        def sem(name):
            return ctx.enter_context(nc.semaphore(name))

        identf, identb = w["identf"], w["identb"]
        wraw = sb("wraw", [P, 3 * E])
        wrope = sb("wrope", [P, 4, P])
        brow = sb("brow", [1, 3 * E])
        brope = sb("brope", [1, 4, P])
        bprow = sb("bprow", [1, E])
        ones = sb("ones", [1, P])
        bcol = sb("bcol", [P, 4])
        bv = sb("bv", [P, E])
        bp = sb("bp", [P, E])
        wp = sb("wp", [P, E])
        gwrow = sb("gwrow", [NEXP, E])
        gwt = sb("gwt", [P, NEXP])
        cos = sb("cos", [P, T])
        sin = sb("sin", [P, T])
        maskf = sb("maskf", [P, P])
        maskb = sb("maskb", [P, P], BF16)
        self_ = sb("self_", [SPLIT * NEXP, NCH * P])
        wraw1 = sb("wraw1", [P, (NCH + 1) * P])
        wraw3 = sb("wraw3", [P, (NCH + 1) * P])
        wraw2 = sb("wraw2", [P, (NCH + 1) * P])
        EXPERT_WEIGHTS = ((wraw1, w["w1h"], w["w1l"]), (wraw3, w["w3h"], w["w3l"]), (wraw2, w["w2h"], w["w2l"]))
        x_in = sb("x_in", [P, TT, E])
        xt = sb("xt", [P, T])
        rope_cos = sb("rope_cos", [P, 2, T])
        rope_sin = sb("rope_sin", [P, 2, T])
        roped = sb("roped", [P, 2, T])
        rest = sb("rest", [P, 2, T])
        parts = sb("parts", [P, 2, SPLIT, T], BF16)
        qs = sb("qs", [P, G, HG * T], BF16)
        ks = sb("ks", [P, G, HG * T], BF16)
        vfresh = sb("vfresh", [P, TT, E])
        vstage = sb("vstage", [P, TT, E])
        v = sb("v", [P, G, TT, HG, 32])
        mx = sb("mx", [P, G, HG, TT])
        negm = sb("negm", [P, SPLIT, HG * TT], BF16)
        mrest = sb("mrest", [P, 2, HG * TT])
        mrows = sb("mrows", [SPLIT * HG * TT, P], BF16)
        probs = sb("probs", [P, 2, B_UNITS, 2 * T])
        ot = sb("ot", [P, T])
        rden = sb("rden", [P, TT, HG])
        o = sb("o", [P, TT, E])
        ot2 = sb("ot2", [P, T])
        xres = sb("xres", [P, TT, E])
        xb = sb("xb", [P, TT, E])
        r = sb("r", [P, TT, E])
        st = sb("st", [P, TT, 6])
        mv = sb("mv", [P, TT, 2])
        small = sb("small", [P, 4, TT])
        x1 = sb("x1", [P, TT, E])
        x1t = sb("x1t", [P, T])
        lmax = sb("lmax", [P, TT])
        z = sb("z", [P, TT, NEXP])
        ez = sb("ez", [P, TT * NEXP])

        bounce = nc.dram_tensor("bounce", [B, 2, NPROD, P, T], BF16, kind="Internal").ap()

        psA = [ctx.enter_context(nc.psum_tensor(f"psA{i}", [P, T], F32)) for i in range(2)]
        psB = [ctx.enter_context(nc.psum_tensor(f"psB{i}", [P, 2 * T], F32)) for i in range(2)]
        psO = ctx.enter_context(nc.psum_tensor("psO", [P, T], F32))
        psM = ctx.enter_context(nc.psum_tensor("psM", [P, T], F32))

        consts_in = sem("consts_in")
        weights_in = sem("weights_in")
        weights_rounded = sem("weights_rounded")
        setup_dve = sem("setup_dve")
        setup_pe = sem("setup_pe")
        setup_pool = sem("setup_pool")
        x_in_loaded = sem("x_in_loaded")
        xres_loaded = sem("xres_loaded")
        parts_ready = sem("parts_ready")
        bounced = sem("bounced")
        qk_loaded = [sem(f"qk_loaded{g}") for g in range(G)]
        mrows_loaded = [sem(f"mrows_loaded{g}") for g in range(G)]
        a_scored = sem("a_scored")
        a_reduced = sem("a_reduced")
        negm_ready = sem("negm_ready")
        b_scored = sem("b_scored")
        exp_done = sem("exp_done")
        causal_done = sem("causal_done")
        pv_done = sem("pv_done")
        ot_copied = sem("ot_copied")
        v_moved = sem("v_moved")
        v_copied = sem("v_copied")
        roped_ready = sem("roped_ready")
        part0_ready = sem("part0_ready")
        rest_ready = sem("rest_ready")
        part1_ready = sem("part1_ready")
        item_full = sem("item_full")
        item_free = sem("item_free")
        xb_ready = sem("xb_ready")
        x1_ready = sem("x1_ready")
        ez_ready = sem("ez_ready")
        x1_stored = sem("x1_stored")
        x1t_stored = sem("x1t_stored")
        ez_stored = sem("ez_stored")
        dve_own = sem("dve_own")

        xv = x.rearrange("b (t p) e -> b p t e", p=P)

        block = ctx.enter_context(nc.Block())

        @block.sync
        def _(sp):
            sp.dma_start(x_in[:, :, :], xv[0]).then_inc(x_in_loaded, 16)
            for dst, src in (
                (identf[:, :], consts[:, C_ID:C_ID + P]), (wraw[:, :], wqkv),
                (brow[:, :], bqkv.rearrange("(a n) -> a n", a=1)), (bprow[:, :], bproj.rearrange("(a n) -> a n", a=1)),
                (gwrow[:, :], gate_w), (cos[:, :], consts[:, C_COS:C_COS + T]), (sin[:, :], consts[:, C_SIN:C_SIN + T]),
                (maskf[:, :], consts[:, C_MASK:C_MASK + P]),
            ):
                sp.dma_start(dst, src).then_inc(consts_in, 16)
            for dst, src in (
                (wp[:, :], wproj), (self_[:, :], consts[0:SPLIT * NEXP, C_SEL:C_L16]),
                (w["less"][:, :], consts[:, C_L16:C_END]),
                (wraw1[:, 0:NEXP * INTER].rearrange("d (e i) -> d e i", e=NEXP), w1.rearrange("e d i -> d e i")),
                (wraw3[:, 0:NEXP * INTER].rearrange("d (e i) -> d e i", e=NEXP), w3.rearrange("e d i -> d e i")),
                (wraw2[:, 0:NCH * E].rearrange("p (c d) -> p c d", c=NCH),
                 w2.rearrange("e i d -> (e i) d").rearrange("(c p) d -> p c d", p=P)),
                (wraw1[:, NCH * P:], ws1), (wraw3[:, NCH * P:], ws3), (wraw2[:, NCH * P:], ws2),
            ):
                sp.dma_start(dst, src).then_inc(weights_in, 16)

            def load_group(b, g):
                wait_alone(sp, bounced, 96 * (b + 1))
                if exists(b, -1):
                    wait_alone(sp, b_scored, 20 * b - 20 + 5 * g + 5)
                for side, dst in ((0, qs), (1, ks)):
                    sp.dma_start(dst[0:KROWS, g, :],
                                 bounce[b, side][:, 32 * g:32 * g + 32, :].rearrange("a (d h) t -> a d (h t)", h=HG)
                                 ).then_inc(qk_loaded[g], 16)

            def load_mrows(b, g, body, item):
                wait_alone(sp, item_free, item_no(body, item))
                sp.dma_start(qs[MROW:MROW + SPLIT, g, :], mrows[:, :]).then_inc(mrows_loaded[g], 16)

            def bounce_parts(b, side):
                wait_alone(sp, parts_ready, 2 * b + side + 1)
                for n in range(SPLIT):
                    rows = bounce[b, 0][n::SPLIT] if side == 0 else bounce[b, 1][SPLIT * n:SPLIT * n + SPLIT]
                    sp.dma_start(rows.rearrange("i p t -> p i t"), parts[:, side, :, :]).then_inc(bounced, 16)

            def step(b):
                if exists(b, 0):
                    load_group(b, 3)
                    load_mrows(b, 1, b, "m1")
                if exists(b, -1):
                    if exists(b, -2):
                        wait_alone(sp, xb_ready, b - 1)
                    sp.dma_start(xres[:, :, :], xv[b - 1]).then_inc(xres_loaded, 16)
                if exists(b, 1):
                    load_group(b + 1, 0)
                if exists(b, 0):
                    load_mrows(b, 2, b, "m2")
                if exists(b, 3):
                    wait_alone(sp, item_full, item_no(b, "xt"))
                    sp.dma_start(x_in[:, :, :], xv[b + 3]).then_inc(x_in_loaded, 16)
                if exists(b, 2):
                    bounce_parts(b + 2, 0)
                if exists(b, 1):
                    load_group(b + 1, 1)
                if exists(b, 0):
                    load_mrows(b, 3, b, "m3")
                if exists(b, 2):
                    bounce_parts(b + 2, 1)
                if exists(b, 1):
                    load_group(b + 1, 2)
                    load_mrows(b + 1, 0, b, "m0")
                if exists(b, -1):
                    wait_alone(sp, x1_ready, b)
                    sp.dma_start(w["x1_d"][b - 1], x1[:, :, :]).then_inc(x1_stored, 16)
                    wait_alone(sp, item_free, item_no(b, "td"))
                    sp.dma_start(w["x1t_d"][b - 1], x1t[:, :]).then_inc(x1t_stored, 16)
                    wait_alone(sp, ez_ready, b)
                    sp.dma_start(w["e_d"][b - 1], ez[:, :]).then_inc(ez_stored, 16)

            run_steps(sp, step)
            sp.wait_ge(x1_stored, 16 * B)
            sp.wait_ge(x1t_stored, 16 * B)
            sp.wait_ge(ez_stored, 16 * B)

        @block.gpsimd
        def _(pool):
            nc.gpsimd.memset(qs[:, :, :].bitcast(F32), 0.0).then_inc(setup_pool, 1)
            nc.gpsimd.memset(ks[:, :, :].bitcast(F32), 0.0).then_inc(setup_pool, 1)
            nc.gpsimd.memset(v[:, :, :, :, :], 0.0).then_inc(setup_pool, 1)
            pool.wait_ge(setup_pool, 3)
            nc.gpsimd.memset(ks[MROW:MROW + SPLIT, :, :], 1.0).then_inc(setup_pool, 1)
            pool.wait_ge(setup_pool, 4)
            nc.gpsimd.memset(v[:, :, :, :, D:D + 1], 1.0).then_inc(setup_pool, 1)
            pool.wait_ge(setup_pool, 5)

            def split(part, b, side):
                n = 2 * (b + 2) + side
                if part == 0:
                    pool.wait_ge(item_free, item_no(b, ("qr", "kr")[side]))
                    nc.gpsimd.tensor_tensor(roped[:, side, :], rope_cos[:, side, :], rope_sin[:, side, :],
                                            ALU.add).then_inc(roped_ready, 1)
                elif part == 1:
                    pool.wait_ge(part0_ready, n + 1)
                    nc.gpsimd.tensor_tensor(rest[:, side, :], roped[:, side, :], parts[:, side, 0, :],
                                            ALU.subtract).then_inc(rest_ready, 1)
                else:
                    pool.wait_ge(part1_ready, n + 1)
                    nc.gpsimd.tensor_tensor(parts[:, side, 2, :], rest[:, side, :], parts[:, side, 1, :],
                                            ALU.subtract).then_inc(parts_ready, 1)

            def causal(ap, heads):
                return nc.gpsimd.affine_select(out=ap, in_=ap, compare_op=ALU.is_ge, fill=0.0, base=0,
                                               pattern=[[0, heads], [1, P]], channel_multiplier=-1)

            def step(b):
                for t in range(G):
                    for u in range(B_UNITS):
                        if exists(b, 0):
                            wait_alone(pool, exp_done, 20 * b + 5 * t + u + 1)
                            unit = probs[:, t % 2, u, :]
                            if u < HG:
                                causal(unit.rearrange("p (a n) -> p a n", n=T)[:, :, 0:P], 2)
                                causal(unit[:, T + 384:2 * T].rearrange("p (a n) -> p a n", a=1), 1).then_inc(causal_done, 1)
                            else:
                                causal(unit.rearrange("p (a n) -> p a n", a=HG)[:, :, 0:P], HG).then_inc(causal_done, 1)
                        for side, first in ((0, 4), (1, 9)):
                            if exists(b, 2) and 5 * t + u - first in (0, 2, 4):
                                split((5 * t + u - first) // 2, b, side)
                        if (t, u) == (1, 1) and exists(b, -1):
                            pool.wait_ge(xres_loaded, 16 * b)
                            if exists(b, -2):
                                pool.wait_ge(item_free, item_no(b - 1, "tc"))
                            nc.gpsimd.tensor_tensor(xb[:, :, :], xres[:, :, :],
                                                    bp[:, :].rearrange("p (a n) -> p a n", a=1).broadcast_to([P, TT, E]),
                                                    ALU.add).then_inc(xb_ready, 1)

            pool.wait_ge(setup_dve, SETUP_DVE)
            for n, (raw, high, low) in enumerate(EXPERT_WEIGHTS):
                pool.wait_ge(weights_rounded, n + 1)
                nc.gpsimd.tensor_tensor(low[:, :], raw[:, :], high[:, :].bitcast(F32), ALU.subtract).then_inc(setup_pool, 1)
            run_steps(pool, step)

        @block.scalar
        def _(act):
            def round_part(part, b, side):
                n = 2 * (b + 2) + side
                if part == 0:
                    act.wait_ge(roped_ready, n + 1)
                    if exists(b, 1):
                        act.wait_ge(bounced, 96 * (b + 2))
                    nc.scalar.copy(parts[:, side, 0, :], roped[:, side, :]).then_inc(part0_ready, 1)
                else:
                    act.wait_ge(rest_ready, n + 1)
                    nc.scalar.copy(parts[:, side, 1, :], rest[:, side, :]).then_inc(part1_ready, 1)

            def copy_v(b, g):
                act.wait_ge(v_moved, b + 1)
                if exists(b, -1):
                    act.wait_ge(pv_done, 4 * b - 4 + g + 1)
                nc.scalar.copy(v[:, g, :, :, 0:D],
                               vstage[:, :, 32 * g:32 * g + 32].rearrange("p t (h d) -> p t h d", d=D)
                               ).then_inc(v_copied, 1)

            def step(b):
                for t in range(G):
                    for u in range(B_UNITS):
                        if exists(b, 0):
                            n = 20 * b + 5 * t + u
                            act.wait_ge(b_scored, n + 1)
                            if t >= 2:
                                act.wait_ge(pv_done, 4 * b + t - 1)
                            elif exists(b, -1):
                                act.wait_ge(pv_done, 4 * b + t - 1)
                            nc.scalar.activation(probs[:, t % 2, u, :], psB[(5 * t + u) % 2][:, :], ACT.Exp,
                                                 scale=SCALE).then_inc(exp_done, 1)
                        if u == 3 and exists(b, 0 if t else -1):
                            act.wait_ge(pv_done, 4 * b + t)
                            before = (b, ("ta3", "ta0", "ta1")[t - 1]) if t else (b - 1, "ta2")
                            if exists(before[0], SHIFT[before[1]]):
                                act.wait_ge(item_full, item_no(*before))
                            nc.scalar.copy(ot[:, :], psO[:, :]).then_inc(ot_copied, 1)
                        if (t, u) == (3, 4) and exists(b, -1):
                            act.wait_ge(item_free, item_no(b, "te"))
                            if exists(b, -2):
                                act.wait_ge(ez_stored, 16 * (b - 1))
                            nc.scalar.activation(ez[:, :], z[:, :, :].rearrange("p t e -> p (t e)"), ACT.Exp).then_inc(ez_ready, 1)
                        item = AT.get((t, u))
                        if item in ("tb", "xt", "td") and exists(b, SHIFT[item]):
                            act.wait_ge(item_full, item_no(b, item))
                            if item == "td" and exists(b, -2):
                                act.wait_ge(x1t_stored, 16 * (b - 1))
                            dst = {"tb": ot2, "xt": xt, "td": x1t}[item]
                            nc.scalar.copy(dst[:, :], psM[:, :]).then_inc(item_free, 1)
                        for side, first in ((0, 5), (1, 10)):
                            if exists(b, 2) and 5 * t + u - first in (0, 2):
                                round_part((5 * t + u - first) // 2, b, side)
                        for at, ahead, g in (((0, 1), 0, 2), ((1, 0), 0, 3), ((2, 1), 1, 0), ((3, 1), 1, 1)):
                            if (t, u) == at and exists(b, ahead):
                                copy_v(b + ahead, g)
                        if (t, u) == (1, 1) and exists(b, 1):
                            act.wait_ge(item_free, item_no(b - 1, "v"))
                            if exists(b, 0):
                                act.wait_ge(v_copied, 4 * b + 4)
                            nc.scalar.copy(vstage[:, :, :], vfresh[:, :, :]).then_inc(v_moved, 1)

            act.wait_ge(weights_in, 16 * 9)
            for raw, high, _ in EXPERT_WEIGHTS:
                nc.scalar.copy(high[:, :], raw[:, :]).then_inc(weights_rounded, 1)
            nc.scalar.copy(w["selb"][:, :, :].rearrange("p c n -> p (c n)"), self_[:, :]).then_inc(weights_rounded, 1)
            act.wait_ge(setup_pool, 5)
            run_steps(act, step)

        @block.tensor
        def _(pe):
            pe.wait_ge(setup_dve, SETUP_BIAS)
            for i in range(4):
                nc.tensor.matmul(psM[:, i:i + 1], brope[0:1, i, :], ones[0:1, 0:1], start=True, stop=True)
            nc.tensor.matmul(psM[:, 8:8 + E], ones[0:1, :], brow[0:1, 2 * E:3 * E], start=True, stop=True)
            nc.tensor.matmul(psM[:, 136:136 + E], ones[0:1, :], bprow[0:1, :], start=True, stop=True)
            nc.tensor.transpose(psM[:, 264:264 + NEXP], gwrow[:, :], identf[0:NEXP, 0:NEXP]).then_inc(setup_pe, 1)
            pe.wait_ge(setup_dve, SETUP_DVE)
            pe.wait_ge(setup_pool, 5)

            def item(b, name):
                no = item_no(b, name)
                if not (isinstance(no, int) and no == 1):
                    wait_alone(pe, item_free, no - 1)
                if name in ("m0", "m1", "m2", "m3"):
                    g = int(name[1])
                    wait_alone(pe, negm_ready, 4 * (b + (g == 0)) + g + 1)
                    last = nc.tensor.transpose(psM[:, :].bitcast(BF16)[0:SPLIT * HG * TT, 0:P],
                                               negm[:, :, :].rearrange("p s n -> p (s n)"), identb[:, :])
                elif name == "xt":
                    pe.wait_ge(x_in_loaded, 16 * (b + 3))
                    for t in range(TT):
                        last = nc.tensor.transpose(psM[:, P * t:P * t + P], x_in[:, t, :], identf[:, :])
                elif name == "v":
                    for t in range(TT):
                        last = nc.tensor.matmul(psM[:, P * t:P * t + P], xt[:, P * t:P * t + P], wraw[:, 2 * E:3 * E],
                                                start=True, stop=True)
                elif name in ("q", "qr", "k", "kr"):
                    last = nc.tensor.matmul(psM[:, :], wrope[:, ("q", "qr", "k", "kr").index(name), :], xt[:, :],
                                            start=True, stop=True)
                elif name[:2] == "ta":
                    g = int(name[2])
                    pe.wait_ge(ot_copied, 4 * (b + SHIFT[name]) + g + 1)
                    for t in range(TT):
                        last = nc.tensor.transpose(psM[:, P * t:P * t + P], ot[:, P * t:P * t + P], identf[:, :])
                elif name == "tb":
                    for t in range(TT):
                        last = nc.tensor.transpose(psM[:, P * t:P * t + P], o[:, t, :], identf[:, :])
                elif name == "tc":
                    pe.wait_ge(weights_in, 16 * 9)
                    for t in range(TT):
                        last = nc.tensor.matmul(psM[:, P * t:P * t + P], ot2[:, P * t:P * t + P], wp[:, :],
                                                start=True, stop=True)
                elif name == "td":
                    pe.wait_ge(x1_ready, b)
                    for t in range(TT):
                        last = nc.tensor.transpose(psM[:, P * t:P * t + P], x1[:, t, :], identf[:, :])
                elif name == "te":
                    for t in range(TT):
                        last = nc.tensor.matmul(psM[:, NEXP * t:NEXP * t + NEXP], x1t[:, P * t:P * t + P], gwt[:, :],
                                                start=True, stop=True)
                last.then_inc(item_full, 1)

            def score_a(b, g, unit):
                if unit < 8:
                    qt, heads = (3, [unit]) if unit < 4 else (2, [unit - 4])
                else:
                    qt, heads = (1, [2 * unit - 16, 2 * unit - 15]) if unit < 10 else (0, range(HG))
                if unit == 0:
                    pe.wait_ge(qk_loaded[g], 32 * (b + 1))
                n = 44 * b + 11 * g + unit
                if not (isinstance(n, int) and n < 2):
                    pe.wait_ge(a_reduced, n - 1)
                bank, width = psA[(11 * g + unit) % 2], P * (qt + 1)
                for i, h in enumerate(heads):
                    nc.tensor.matmul(bank[:, width * i:width * i + width],
                                     qs[0:KA, g, T * h + P * qt:T * h + P * qt + P], ks[0:KA, g, T * h:T * h + width],
                                     start=True, stop=False)
                    last = nc.tensor.matmul(bank[:, width * i + width - P:width * i + width], identb[:, :], maskb[:, :],
                                            start=False, stop=True)
                last.then_inc(a_scored, 1)

            def score_b(b, g, u):
                n = 20 * b + 5 * g + u
                if u == 0:
                    pe.wait_ge(mrows_loaded[g], 16 * (b + 1))
                if not (isinstance(n, int) and n < 2):
                    pe.wait_ge(exp_done, n - 1)
                dst = psB[(5 * g + u) % 2]
                if u < HG:
                    todo = [(T * u, 0, 0), (T * u, 1, T), (T * u, 3, T + 384)]
                else:
                    todo = [(T * h, 2, 256 * h) for h in range(HG)]
                for at, kt, col in todo:
                    last = nc.tensor.matmul(dst[:, col:col + T - P * kt], ks[:, g, at + P * kt:at + P * kt + P],
                                            qs[:, g, at + P * kt:at + T], start=True, stop=True)
                last.then_inc(b_scored, 1)

            def weigh(b, g, part):
                kt = (0, 1, 3, 2)[part]
                if part == 0:
                    if not (isinstance(b, int) and 4 * b + g < 1):
                        pe.wait_ge(ot_copied, 4 * b + g)
                    pe.wait_ge(v_copied, 4 * b + g + 1)
                for h in range(HG):
                    if part == 0:
                        pe.wait_ge(causal_done, 20 * b + 5 * g + h + 1)
                    if part == 3 and h == 0:
                        pe.wait_ge(causal_done, 20 * b + 5 * g + 5)
                    unit, at = (h, (0, T, 0, T + 384)[kt]) if kt != 2 else (HG, 256 * h)
                    last = nc.tensor.matmul(psO[32 * h:32 * h + 32, P * kt:T], v[:, g, kt, h, :],
                                            probs[:, g % 2, unit, at:at + T - P * kt],
                                            start=(part == 0), stop=(part == 3))
                if part == 3:
                    last.then_inc(pv_done, 1)

            def step(b):
                for t in range(G):
                    for u in range(B_UNITS):
                        if exists(b, 0):
                            score_b(b, t, u)
                        ahead, ga = (0, t + 2) if t < 2 else (1, t - 2)
                        if exists(b, ahead):
                            for unit in range(*A_SPLIT[u]):
                                score_a(b + ahead, ga, unit)
                        back, gp = (0, t - 1) if t else (-1, 3)
                        if u < 4 and exists(b, back):
                            weigh(b + back, gp, u)
                        name = AT.get((t, u))
                        if name and exists(b, SHIFT[name]):
                            item(b, name)

            run_steps(pe, step)

        @block.vector
        def _(dve):
            chain = Chain(dve, dve_own)
            chain.per = 4 * 3 + 4 + 1 + NORM_CHAIN
            dve.wait_ge(consts_in, 16 * 8)
            nc.vector.tensor_copy(identb[:, :], identf[:, :]).then_inc(setup_dve, 1)
            nc.vector.memset(ones[:, :], 1.0).then_inc(setup_dve, 1)

            def spread(dst, src):
                plain = dst[:, 0, :].rearrange("p (g d h) -> p g h d", g=G, d=D)
                turned = dst[:, 1, :].rearrange("p (g d two h) -> p g h d two", g=G, d=D // 2, two=2)
                given = src.rearrange("p (g h d) -> p g h d", g=G, h=HG)
                pairs = src.rearrange("p (g h d two) -> p g h d two", g=G, h=HG, two=2)
                for g in range(G):
                    nc.vector.tensor_copy(plain[:, g], given[:, g])
                    nc.vector.tensor_scalar(turned[:, g, :, :, 0], pairs[:, g, :, :, 1], -1.0, None, ALU.mult)
                    last = nc.vector.tensor_copy(turned[:, g, :, :, 1], pairs[:, g, :, :, 0])
                last.then_inc(setup_dve, 1)

            for side in range(2):
                spread(wrope[:, 2 * side:2 * side + 2, :], wraw[:, E * side:E * side + E])
                spread(brope[:, 2 * side:2 * side + 2, :], brow[:, E * side:E * side + E])
            nc.vector.tensor_copy(maskb[:, :], maskf[:, :]).then_inc(setup_dve, 1)
            nc.vector.memset(st[:, :, :], 0.0).then_inc(setup_dve, 1)
            dve.wait_ge(setup_pe, 1)
            nc.vector.tensor_copy(bcol[:, :], psM[:, 0:4]).then_inc(setup_dve, 1)
            nc.vector.tensor_copy(bv[:, :], psM[:, 8:8 + E]).then_inc(setup_dve, 1)
            nc.vector.tensor_copy(bp[:, :], psM[:, 136:136 + E]).then_inc(setup_dve, 1)
            nc.vector.tensor_copy(gwt[:, :], psM[:, 264:264 + NEXP]).then_inc(setup_dve, 1)
            nc.vector.memset(small[:, :, :], 0.0).then_inc(setup_dve, 1)
            nc.vector.memset(mv[:, :, :], 0.0).then_inc(setup_dve, 1)
            dve.wait_ge(setup_dve, SETUP_DVE)

            def reduce_a(b, g, unit):
                dve.wait_ge(a_scored, 44 * b + 11 * g + unit + 1)
                bank = psA[(11 * g + unit) % 2]
                if unit < 8:
                    qt, h0, n = (3, unit, 1) if unit < 4 else (2, unit - 4, 1)
                else:
                    qt, h0, n = (1, 2 * unit - 16, 2) if unit < 10 else (0, 0, HG)
                width = P * (qt + 1)
                nc.vector.tensor_reduce(mx[:, g, h0:h0 + n, qt],
                                        bank[:, 0:width * n].rearrange("p (a n) -> p a n", a=n),
                                        AX_X, ALU.max).then_inc(a_reduced, 1)

            def split_max(b, g):
                dve.wait_ge(a_reduced, 44 * b + 11 * g + 11)
                m = mx[:, g, :, :].rearrange("p h t -> p (h t)")
                chain(nc.vector.tensor_scalar(negm[:, 0, :], m, -1.0, None, ALU.mult))
                chain.wait()
                chain(nc.vector.scalar_tensor_tensor(out=mrest[:, 0, :], in0=m, scalar=-1.0, in1=negm[:, 0, :],
                                                     op0=ALU.mult, op1=ALU.subtract))
                chain.wait()
                chain(nc.vector.tensor_copy(negm[:, 1, :], mrest[:, 0, :]))
                chain.wait()
                nc.vector.tensor_tensor(negm[:, 2, :], mrest[:, 0, :], negm[:, 1, :], ALU.subtract).then_inc(negm_ready, 1)

            def item(b, name):
                dve.wait_ge(item_full, item_no(b, name))
                if name in ("m0", "m1", "m2", "m3"):
                    g = int(name[1])
                    if g:
                        dve.wait_ge(mrows_loaded[g - 1], 16 * (b + 1))
                    elif exists(b, 0):
                        dve.wait_ge(mrows_loaded[3], 16 * (b + 1))
                    nc.vector.tensor_copy(mrows[:, :], psM[:, :].bitcast(BF16)[0:SPLIT * HG * TT, 0:P]).then_inc(item_free, 1)
                elif name == "v":
                    if exists(b, 1):
                        dve.wait_ge(v_moved, b + 2)
                    nc.vector.tensor_tensor(vfresh[:, :, :], psM[:, :].rearrange("p (t e) -> p t e", t=TT),
                                            bv[:, :].rearrange("p (a n) -> p a n", a=1).broadcast_to([P, TT, E]),
                                            ALU.add).then_inc(item_free, 1)
                elif name in ("q", "qr", "k", "kr"):
                    side, turned = name[0] == "k", len(name) == 2
                    if not turned and exists(b, 1):
                        dve.wait_ge(roped_ready, 2 * (b + 2) - 1 + side)
                    dst, table = (rope_sin, sin) if turned else (rope_cos, cos)
                    nc.vector.scalar_tensor_tensor(out=dst[:, int(side), :], in0=psM[:, :],
                                                   scalar=bcol[:, 2 * side + turned:2 * side + turned + 1],
                                                   in1=table[:, :], op0=ALU.add, op1=ALU.mult).then_inc(item_free, 1)
                elif name[:2] == "ta":
                    g = int(name[2])
                    got = psM[:, :].rearrange("p (t h c) -> p t h c", t=TT, h=HG)
                    chain(nc.vector.reciprocal(rden[:, :, :], got[:, :, :, D]))
                    chain.wait()
                    nc.vector.tensor_tensor(o[:, :, 32 * g:32 * g + 32].rearrange("p t (h d) -> p t h d", h=HG),
                                            got[:, :, :, 0:D],
                                            rden[:, :, :].rearrange("p t (h a) -> p t h a", a=1).broadcast_to([P, TT, HG, D]),
                                            ALU.mult).then_inc(item_free, 1)
                elif name == "tc":
                    dve.wait_ge(xb_ready, b)
                    nc.vector.tensor_tensor(r[:, :, :], psM[:, :].rearrange("p (t e) -> p t e", t=TT), xb[:, :, :],
                                            ALU.add).then_inc(item_free, 1)
                elif name == "te":
                    logits = psM[:, 0:TT * NEXP].rearrange("p (t e) -> p t e", t=TT)
                    chain(nc.vector.tensor_reduce(lmax[:, :], logits, AX_X, ALU.max))
                    chain.wait()
                    if exists(b, -2):
                        dve.wait_ge(ez_ready, b - 1)
                    nc.vector.tensor_tensor(z[:, :, :], logits,
                                            lmax[:, :].rearrange("p (t a) -> p t a", a=1).broadcast_to([P, TT, NEXP]),
                                            ALU.subtract).then_inc(item_free, 1)

            def step(b):
                for t in range(G):
                    for u in range(B_UNITS):
                        ahead, gm = (0, t + 1) if t < 3 else (1, 0)
                        if u == 0 and exists(b, ahead):
                            split_max(b + ahead, gm)
                        ahead, ga = (0, t + 2) if t < 2 else (1, t - 2)
                        if exists(b, ahead):
                            for unit in range(*A_SPLIT[u]):
                                reduce_a(b + ahead, ga, unit)
                        name = AT.get((t, u))
                        if name and name not in ("tb", "xt", "td") and exists(b, SHIFT[name]):
                            item(b, name)
                        if exists(b, -1):
                            if (t, u) == (2, 2):
                                dve.wait_ge(item_free, item_no(b, "tc"))
                                norm_moments(nc, chain, r, st, mv)
                            if (t, u) == (2, 3):
                                norm_rsqrt(nc, chain, mv, small)
                            if (t, u) == (3, 0):
                                if exists(b, -2):
                                    dve.wait_ge(x1_stored, 16 * (b - 1))
                                norm_apply(nc, chain, r, x1, mv, small, x1_ready)

            run_steps(dve, step, chain)


def expert_pass(nc, w, out):
    NC1 = NCH + 1
    ctx = ExitStack()
    with ctx:
        def sb(name, shape, dt=F32):
            return ctx.enter_context(nc.sbuf_tensor(name, shape, dt))

        def sem(name):
            return ctx.enter_context(nc.semaphore(name))

        identf, identb = w["identf"], w["identb"]
        less16 = w["less"][:, 0:NEXP * NEXP].rearrange("p (e f) -> p e f", e=NEXP)
        less4 = w["less"][:, NEXP * NEXP:].rearrange("p (e f) -> p e f", e=NGRP)

        x1 = [sb(f"x1_{i}", [P, TT, E]) for i in range(2)]
        x1t = [sb(f"x1t_{i}", [P, T]) for i in range(2)]
        xh = [sb(f"xh_{i}", [P, T], F32R) for i in range(2)]
        xl = [sb(f"xl_{i}", [P, T], F32R) for i in range(2)]
        ez = sb("ez2", [P, TT, NEXP])
        ct = [sb(f"ct_{i}", [SPLIT * NEXP, T], BF16) for i in range(2)]
        esum = sb("esum", [P, TT])
        erec = sb("erec", [P, TT])
        score = sb("score", [P, TT, NEXP])
        gmax = sb("gmax", [P, TT, NGRP])
        gd = sb("gd", [P, TT, NGRP, NGRP])
        ge = sb("ge", [P, TT, NGRP, NGRP])
        grank = sb("grank", [P, TT, NGRP])
        masked = sb("masked", [P, TT, NEXP])
        ed = sb("ed", [P, TT, NEXP, NEXP])
        ee = sb("ee", [P, TT, NEXP, NEXP])
        erank = sb("erank", [P, TT, NEXP])
        c = sb("c", [P, TT, NEXP])
        crest = sb("crest", [P, TT, NEXP])
        cparts = sb("cparts", [P, TT, SPLIT, NEXP], BF16)
        s = [sb(f"s_{i}", [P, T]) for i in range(2)]
        sh = [sb(f"sh_{i}", [P, T]) for i in range(2)]
        a = [sb(f"a_{i}", [P, T]) for i in range(2)]
        ah = [sb(f"ah_{i}", [P, T], F32R) for i in range(3)]
        al = [sb(f"al_{i}", [P, T], F32R) for i in range(3)]
        yt = sb("yt", [P, T])
        r = sb("r2", [P, TT, E])
        st = sb("st2", [P, TT, 6])
        mv = sb("mv2", [P, TT, 2])
        small = sb("small2", [P, 4, TT])
        res = sb("res", [P, TT, E])

        psH1 = [ctx.enter_context(nc.psum_tensor(f"psH1_{i}", [P, T], F32)) for i in range(2)]
        psH3 = [ctx.enter_context(nc.psum_tensor(f"psH3_{i}", [P, T], F32)) for i in range(2)]
        psC = [ctx.enter_context(nc.psum_tensor(f"psC_{i}", [P, T], F32)) for i in range(2)]
        psY = ctx.enter_context(nc.psum_tensor("psY", [P, T], F32))
        psM = ctx.enter_context(nc.psum_tensor("psM2", [P, T], F32))

        x1_loaded = [sem(f"x1_loaded{i}") for i in range(2)]
        x1t_loaded = [sem(f"x1t_loaded{i}") for i in range(2)]
        ez_loaded = sem("ez_loaded")
        xh_ready = sem("xh_ready")
        xl_ready = sem("xl_ready")
        masked_ready = sem("masked_ready")
        ed_ready = sem("ed_ready")
        cparts_ready = sem("cparts_ready")
        ct_transposed = sem("ct_transposed")
        ct_copied = sem("ct_copied")
        h1_ready = sem("h1_ready")
        hc_ready = sem("hc_ready")
        silu_ready = sem("silu_ready")
        a_ready = sem("a_ready")
        ah_ready = sem("ah_ready")
        al_ready = sem("al_ready")
        y_added = sem("y_added")
        yt_copied = sem("yt_copied")
        y_turned = sem("y_turned")
        y_taken = sem("y_taken")
        res_ready = sem("res_ready")
        out_stored = sem("out_stored")
        own = sem("dve_own2")

        ov = out.rearrange("b (t p) e -> b p t e", p=P)
        block = ctx.enter_context(nc.Block())

        def run_pairs(engine, step, chain=None):
            step(0, 0)
            step(1, 1)
            if chain is not None:
                done, chain.n = chain.n, 0
            with engine.Fori(1, B // 2 - 1) as i:
                for par in range(2):
                    if chain is not None and par == 0:
                        chain.base = i * (2 * chain.per) + (done - 2 * chain.per)
                    step(i * 2 + par, par)
            if chain is not None:
                assert chain.n == 2 * chain.per, chain.n
                chain.base, chain.n = 0, done + 2 * chain.per * (B // 2 - 2)
            step(B - 2, 0)
            step(B - 1, 1)

        def first(b):
            return isinstance(b, int) and b == 0

        def last_batch(b):
            return isinstance(b, int) and b == B - 1

        def from_chunk(n, start):
            return not isinstance(n, int) or n >= start

        def nth(par, ch):
            return NC1 * par + ch

        @block.sync
        def _(sp):
            def load(b, par):
                if not first(b):
                    wait_alone(sp, cparts_ready, b)
                sp.dma_start(ez[:, :, :], w["e_d"][b].rearrange("p (t e) -> p t e", t=TT)).then_inc(ez_loaded, 16)
                if not (isinstance(b, int) and b < 2):
                    wait_alone(sp, xl_ready, b - 1)
                sp.dma_start(x1t[par][:, :], w["x1t_d"][b]).then_inc(x1t_loaded[par], 16)
                if not (isinstance(b, int) and b < 2):
                    wait_alone(sp, y_taken, b - 1)
                sp.dma_start(x1[par][:, :, :], w["x1_d"][b]).then_inc(x1_loaded[par], 16)

            def step(b, par):
                if not last_batch(b):
                    load(b + 1, 1 - par)
                if not first(b):
                    wait_alone(sp, res_ready, b)
                    sp.dma_start(ov[b - 1], res[:, :, :]).then_inc(out_stored, 16)

            load(0, 0)
            run_pairs(sp, step)
            sp.wait_ge(res_ready, B)
            sp.dma_start(ov[B - 1], res[:, :, :]).then_inc(out_stored, 16)
            sp.wait_ge(out_stored, 16 * B)

        @block.gpsimd
        def _(pool):
            def low_x(b, par):
                pool.wait_ge(xh_ready, b + 1)
                nc.gpsimd.tensor_tensor(xl[par][:, :], x1t[par][:, :], xh[par][:, :].bitcast(F32),
                                        ALU.subtract).then_inc(xl_ready, 1)

            def expert_differences(b):
                pool.wait_ge(masked_ready, b + 1)
                nc.gpsimd.tensor_tensor(
                    ed[:, :, :, :], masked[:, :, :].rearrange("p t (a f) -> p t a f", a=1).broadcast_to([P, TT, NEXP, NEXP]),
                    masked[:, :, :].rearrange("p t (e a) -> p t e a", a=1).broadcast_to([P, TT, NEXP, NEXP]),
                    ALU.subtract).then_inc(ed_ready, 1)

            def step(b, par):
                for ch in range(NC1):
                    n, k = NC1 * b + ch, nth(par, ch)
                    pool.wait_ge(ah_ready, n + 1)
                    nc.gpsimd.tensor_tensor(al[k % 3][:, :], a[k % 2][:, :], ah[k % 3][:, :].bitcast(F32),
                                            ALU.subtract).then_inc(al_ready, 1)
                    if ch == 2 and not last_batch(b):
                        expert_differences(b + 1)
                    if ch == 5 and not last_batch(b):
                        low_x(b + 1, 1 - par)

            low_x(0, 0)
            expert_differences(0)
            run_pairs(pool, step)

        @block.scalar
        def _(act):
            def high_x(b, par):
                act.wait_ge(x1t_loaded[par], (b - par) * 8 + 16)
                if not (isinstance(b, int) and b < 2):
                    act.wait_ge(hc_ready, NC1 * (b - 1))
                nc.scalar.copy(xh[par][:, :], x1t[par][:, :]).then_inc(xh_ready, 1)

            def copy_ct(b, par):
                act.wait_ge(ct_transposed, b + 1)
                nc.scalar.copy(ct[par][:, :], psM[:, :].bitcast(BF16)[0:SPLIT * NEXP, 0:T]).then_inc(ct_copied, 1)

            def copy_y(b):
                act.wait_ge(y_added, NC1 * b + NC1)
                nc.scalar.copy(yt[:, :], psY[:, :]).then_inc(yt_copied, 1)

            def silu(b, par, ch):
                n, k = NC1 * b + ch, nth(par, ch)
                act.wait_ge(h1_ready, n + 1)
                if from_chunk(n, 2):
                    act.wait_ge(a_ready, n - 1)
                nc.scalar.activation(s[k % 2][:, :], psH1[k % 2][:, :], ACT.Silu).then_inc(silu_ready, 1)

            def high_a(b, par, ch):
                n, k = NC1 * b + ch, nth(par, ch)
                act.wait_ge(a_ready, n + 1)
                if from_chunk(n, 3):
                    act.wait_ge(y_added, n - 2)
                nc.scalar.copy(ah[k % 3][:, :], a[k % 2][:, :]).then_inc(ah_ready, 1)

            def step(b, par):
                for ch in range(NC1):
                    silu(b, par, ch)
                    if ch:
                        high_a(b, par, ch - 1)
                    elif not first(b):
                        high_a(b - 1, 1 - par, NCH)
                    if ch == 2 and not first(b):
                        copy_y(b - 1)
                    if ch == 4 and not last_batch(b):
                        high_x(b + 1, 1 - par)
                    if ch == 8 and not last_batch(b):
                        copy_ct(b + 1, 1 - par)

            high_x(0, 0)
            copy_ct(0, 0)
            run_pairs(act, step)
            high_a(B - 1, 1, NCH)
            copy_y(B - 1)

        @block.tensor
        def _(pe):
            def turn_c(b, par):
                if not first(b):
                    pe.wait_ge(ct_copied, b)
                if not (isinstance(b, int) and b < 2):
                    pe.wait_ge(y_taken, b - 1)
                wait_alone(pe, cparts_ready, b + 1)
                for t in range(TT):
                    last = nc.tensor.transpose(psM[:, :].bitcast(BF16)[0:SPLIT * NEXP, P * t:P * t + P],
                                               cparts[:, t, :, :].rearrange("p s e -> p (s e)"), identb[:, :])
                last.then_inc(ct_transposed, 1)

            def turn_y(b):
                pe.wait_ge(yt_copied, b + 1)
                pe.wait_ge(ct_copied, b + 2 if not (isinstance(b, int) and b + 2 > B) else B)
                for t in range(TT):
                    last = nc.tensor.transpose(psM[:, P * t:P * t + P], yt[:, P * t:P * t + P], identf[:, :])
                last.then_inc(y_turned, 1)

            def product(dst, high, low, right_high, right_low, start=True, stop=True):
                nc.tensor.matmul(dst, high, right_high, start=start, stop=False)
                nc.tensor.matmul(dst, high, right_low, start=False, stop=False)
                return nc.tensor.matmul(dst, low, right_high, start=False, stop=stop)

            def hidden(b, par, ch):
                n, k = NC1 * b + ch, nth(par, ch)
                at = slice(P * ch, P * ch + P)
                if from_chunk(n, 2):
                    pe.wait_ge(a_ready, n - 1)
                product(psH1[k % 2][:, :], w["w1h"][:, at], w["w1l"][:, at], xh[par][:, :], xl[par][:, :]).then_inc(h1_ready, 1)
                last = product(psH3[k % 2][:, :], w["w3h"][:, at], w["w3l"][:, at], xh[par][:, :], xl[par][:, :])
                if ch < NCH:
                    last = nc.tensor.matmul(psC[k % 2][:, :], w["selb"][:, ch, :], ct[par][:, :], start=True, stop=True)
                last.then_inc(hc_ready, 1)

            def down(b, par, ch):
                n, k = NC1 * b + ch, nth(par, ch)
                at = slice(P * ch, P * ch + P)
                pe.wait_ge(al_ready, n + 1)
                if ch == 0 and not first(b):
                    pe.wait_ge(yt_copied, b)
                product(psY[:, :], w["w2h"][:, at], w["w2l"][:, at], ah[k % 3][:, :], al[k % 3][:, :],
                        start=(ch == 0), stop=(ch == NCH)).then_inc(y_added, 1)

            def step(b, par):
                pe.wait_ge(xl_ready, b + 1)
                pe.wait_ge(ct_copied, b + 1)
                for ch in range(NC1):
                    hidden(b, par, ch)
                    if ch > 1:
                        down(b, par, ch - 2)
                    elif not first(b):
                        down(b - 1, 1 - par, NCH - 1 + ch)
                    if ch == 3 and not first(b):
                        turn_y(b - 1)
                    if ch == 8 and not last_batch(b):
                        turn_c(b + 1, 1 - par)

            turn_c(0, 0)
            run_pairs(pe, step)
            down(B - 1, 1, NCH - 1)
            down(B - 1, 1, NCH)
            turn_y(B - 1)

        @block.vector
        def _(dve):
            chain = Chain(dve, own)
            chain.per = NCH + 4 + 4 + 3 + 1 + 3 + NORM_CHAIN

            def bcast(ap, shape):
                return ap.broadcast_to(shape)

            def comes_before(diff, before, result, less, n, part):
                if part == 0:
                    chain(nc.vector.scalar_tensor_tensor(
                        out=before[:, :, :, :], in0=diff[:, :, :, :], scalar=0.0,
                        in1=bcast(less.rearrange("p (a e) f -> p a e f", a=1), [P, TT, n, n]), op0=ALU.is_equal, op1=ALU.mult))
                elif part == 1:
                    chain(nc.vector.scalar_tensor_tensor(
                        out=before[:, :, :, :], in0=diff[:, :, :, :], scalar=0.0, in1=before[:, :, :, :],
                        op0=ALU.is_gt, op1=ALU.add))
                else:
                    chain(nc.vector.tensor_reduce(result[:, :, :], before[:, :, :, :], AX_X, ALU.add))
                chain.wait()

            def router_scores(b):
                dve.wait_ge(ez_loaded, 16 * (b + 1))
                chain(nc.vector.tensor_reduce(esum[:, :], ez[:, :, :], AX_X, ALU.add))
                chain.wait()
                chain(nc.vector.reciprocal(erec[:, :], esum[:, :]))
                chain.wait()
                chain(nc.vector.tensor_tensor(score[:, :, :], ez[:, :, :],
                                              bcast(erec[:, :].rearrange("p (t a) -> p t a", a=1), [P, TT, NEXP]), ALU.mult))
                chain.wait()
                chain(nc.vector.tensor_reduce(gmax[:, :, :].rearrange("p t g -> p (t g)"),
                                              score[:, :, :].rearrange("p t (g e) -> p (t g) e", g=NGRP), AX_X, ALU.max))
                chain.wait()

            def router_groups(b):
                chain(nc.vector.tensor_tensor(
                    gd[:, :, :, :], bcast(gmax[:, :, :].rearrange("p t (a f) -> p t a f", a=1), [P, TT, NGRP, NGRP]),
                    bcast(gmax[:, :, :].rearrange("p t (e a) -> p t e a", a=1), [P, TT, NGRP, NGRP]), ALU.subtract))
                chain.wait()
                for part in range(3):
                    comes_before(gd, ge, grank, less4, NGRP, part)
                nc.vector.scalar_tensor_tensor(
                    out=masked[:, :, :].rearrange("p t (g e) -> p (t g) e", g=NGRP),
                    in0=bcast(grank[:, :, :].rearrange("p t (g a) -> p (t g) a", a=1), [P, TT * NGRP, EPG]),
                    scalar=TOP_GROUPS - 0.5, in1=score[:, :, :].rearrange("p t (g e) -> p (t g) e", g=NGRP),
                    op0=ALU.is_lt, op1=ALU.mult).then_inc(masked_ready, 1)

            def router_experts(b):
                chain(nc.vector.scalar_tensor_tensor(out=c[:, :, :], in0=erank[:, :, :], scalar=TOP_EXPERTS - 0.5,
                                                     in1=score[:, :, :], op0=ALU.is_lt, op1=ALU.mult))
                chain.wait()
                if not first(b):
                    dve.wait_ge(ct_transposed, b)
                chain(nc.vector.tensor_copy(cparts[:, :, 0, :], c[:, :, :]))
                chain.wait()
                chain(nc.vector.tensor_tensor(crest[:, :, :], c[:, :, :], cparts[:, :, 0, :], ALU.subtract))
                chain.wait()
                chain(nc.vector.tensor_copy(cparts[:, :, 1, :], crest[:, :, :]))
                chain.wait()
                nc.vector.tensor_tensor(cparts[:, :, 2, :], crest[:, :, :], cparts[:, :, 1, :],
                                        ALU.subtract).then_inc(cparts_ready, 1)

            def residual(b, par):
                dve.wait_ge(y_turned, b + 1)
                dve.wait_ge(x1_loaded[par], (b - par) * 8 + 16)
                if not first(b):
                    dve.wait_ge(res_ready, b)
                nc.vector.tensor_tensor(r[:, :, :], psM[:, :].rearrange("p (t e) -> p t e", t=TT), x1[par][:, :, :],
                                        ALU.add).then_inc(y_taken, 1)
                dve.wait_ge(y_taken, b + 1)

            def normalise(b):
                if not first(b):
                    dve.wait_ge(out_stored, 16 * b)
                norm_apply(nc, chain, r, res, mv, small, res_ready)

            def step(b, par):
                for ch in range(NC1):
                    n, k = NC1 * b + ch, nth(par, ch)
                    dve.wait_ge(silu_ready, n + 1)
                    dve.wait_ge(hc_ready, n + 1)
                    dst = a[k % 2][:, :]
                    if ch < NCH:
                        chain(nc.vector.tensor_tensor(sh[k % 2][:, :], s[k % 2][:, :], psH3[k % 2][:, :], ALU.mult))
                        chain.wait()
                        if from_chunk(n, 2):
                            dve.wait_ge(al_ready, n - 1)
                        nc.vector.tensor_tensor(dst, sh[k % 2][:, :], psC[k % 2][:, :], ALU.mult).then_inc(a_ready, 1)
                    else:
                        dve.wait_ge(al_ready, n - 1)
                        nc.vector.tensor_tensor(dst, s[k % 2][:, :], psH3[k % 2][:, :], ALU.mult).then_inc(a_ready, 1)
                    if not last_batch(b):
                        if ch == 0:
                            router_scores(b + 1)
                        if ch == 1:
                            router_groups(b + 1)
                        if ch in (4, 5, 6):
                            if ch == 4:
                                dve.wait_ge(ed_ready, b + 2)
                            comes_before(ed, ee, erank, less16, NEXP, ch - 4)
                        if ch == 7:
                            router_experts(b + 1)
                    if not first(b):
                        if ch == 3:
                            residual(b - 1, 1 - par)
                            norm_moments(nc, chain, r, st, mv)
                        if ch == 7:
                            norm_rsqrt(nc, chain, mv, small)
                        if ch == 8:
                            normalise(b - 1)

            router_scores(0)
            router_groups(0)
            dve.wait_ge(ed_ready, 1)
            for part in range(3):
                comes_before(ed, ee, erank, less16, NEXP, part)
            router_experts(0)
            run_pairs(dve, step, chain)
            residual(B - 1, 1)
            norm_moments(nc, chain, r, st, mv)
            norm_rsqrt(nc, chain, mv, small)
            normalise(B - 1)


_INS = ["L0_attn_x", "L0_attn_Wqkv", "L0_attn_bqkv", "L0_attn_Wproj", "L0_attn_bproj", "L0_ffn_gate_w",
        "L0_ffn_w1", "L0_ffn_w2", "L0_ffn_w3", "L0_ffn_ws1", "L0_ffn_ws2", "L0_ffn_ws3"]
_OUTS = [((B, T, E), "float32")]


def kernel(**inputs):
    import concourse.bacc as _bacc
    from concourse.bass_utils import run_bass_kernel_spmd as _run

    nc = _bacc.Bacc("TRN2", target_bir_lowering=False, num_devices=1)
    arrays, args = {}, []
    for name in _INS:
        arrays[f"in_{name}"] = np.ascontiguousarray(inputs[name])
    arrays["in_constants"] = constants()
    for name, a in arrays.items():
        args.append(nc.dram_tensor(name, a.shape, mybir.dt.from_np(a.dtype), kind="ExternalInput").ap())
    for i, (shape, dtype) in enumerate(_OUTS):
        args.append(nc.dram_tensor(f"out_{i}", shape, mybir.dt.from_np(np.dtype(dtype)), kind="ExternalOutput").ap())
    layer_kernel(nc, *args)
    r = _run(nc, [arrays], core_ids=[0])
    return r.results[0]["out_0"]
```

```python
from contextlib import ExitStack

import numpy as np

import concourse.bass as bass
from concourse import mybir

ALU = mybir.AluOpType
ACT = mybir.ActivationFunctionType
F32 = mybir.dt.float32
F32R = mybir.dt.float32r
BF16 = mybir.dt.bfloat16
I32 = mybir.dt.int32
AX_X = mybir.AxisListType.X

P = 128
B, T, E = 16, 512, 128
H, D = 16, 8
G, HG = 4, 4
TT = T // P
assert H == G * HG
SPLIT = 3
NPROD = SPLIT * SPLIT
KROWS = NPROD * D
KA = 96
MROW = 96
NEXP, INTER = 16, 64
NCH = NEXP * INTER // P
NGRP, EPG = 4, 4
TOP_GROUPS, TOP_EXPERTS = 2, 4
SCALE = float(D) ** -0.5
EPS = 1e-5
MASKED = -3.0e38

BF16_ONES = float(np.uint32(0x3F803F80).view(np.float32))
SETUP_DVE = 19
SETUP_BIAS = 11
A_UNITS = 11
B_UNITS = 5
A_SPLIT = [(0, 2), (2, 4), (4, 6), (6, 8), (8, A_UNITS)]

C_ID, C_COS, C_SIN, C_MASK = 0, P, P + T, P + 2 * T
C_SEL = C_MASK + P
C_L16 = C_SEL + NCH * P
C_L4 = C_L16 + NEXP * NEXP
C_END = C_L4 + NGRP * NGRP


def constants():
    c = np.zeros((P, C_END), np.float32)
    c[:, C_ID:C_ID + P] = np.eye(P, dtype=np.float32)
    inv_freq = (np.float32(1.0) / np.float32(10000.0) ** (np.arange(0, D, 2, dtype=np.float32) / np.float32(D)))
    freqs = np.arange(T, dtype=np.float32)[None, :] * inv_freq.astype(np.float32)[:, None]
    channel_d = (np.arange(P) // HG) % D
    c[:, C_COS:C_COS + T] = np.cos(freqs)[channel_d // 2]
    c[:, C_SIN:C_SIN + T] = np.sin(freqs)[channel_d // 2]
    c[:, C_MASK:C_MASK + P] = np.triu(np.full((P, P), MASKED, np.float32), 1)
    for s in range(SPLIT):
        for e in range(NEXP):
            ch, half = divmod(e, 2)
            at = C_SEL + ch * P + half * INTER
            c[s * NEXP + e, at:at + INTER] = 1.0
    c[:, C_L16:C_L4] = np.tril(np.ones((NEXP, NEXP), np.float32), -1).reshape(1, -1)
    c[:, C_L4:C_END] = np.tril(np.ones((NGRP, NGRP), np.float32), -1).reshape(1, -1)
    return c


ITEMS = [("xt", 2), ("m1", 0), ("q", 2), ("qr", 2), ("ta3", -1), ("k", 2), ("m2", 0), ("kr", 2), ("tb", -1),
         ("ta0", 0), ("tc", -1), ("m3", 0), ("v", 2), ("ta1", 0), ("m0", 1), ("td", -1), ("te", -1), ("ta2", 0)]
AT = {(0, 0): "xt", (0, 1): "m1", (0, 2): "q", (0, 3): "qr", (0, 4): "ta3", (1, 0): "k", (1, 1): "m2",
      (1, 2): "kr", (1, 3): "tb", (1, 4): "ta0", (2, 0): "tc", (2, 1): "m3", (2, 2): "v", (2, 4): "ta1",
      (3, 1): "m0", (3, 2): "td", (3, 3): "te", (3, 4): "ta2"}
SHIFT = dict(ITEMS)
ORDER = [n for n, _ in ITEMS]
LOOP = range(3, B - 3)


def exists(b, shift):
    return not isinstance(b, int) or 0 <= b + shift < B


def item_no(b, name):
    if isinstance(b, int):
        before = sum(exists(s, sh) for s in range(-2, b) for _, sh in ITEMS)
        return before + sum(exists(b, SHIFT[n]) for n in ORDER[:ORDER.index(name) + 1])
    return b * len(ITEMS) + (item_no(LOOP[0], name) - LOOP[0] * len(ITEMS))


def wait_alone(engine, semaphore, value):
    if not isinstance(value, int):
        value = engine.to_reg(value)
        engine.wait_ge(semaphore, 1)
    engine.wait_ge(semaphore, value)


NEWTON = 3
ROUTER_START, ROUTER_GROUPS, ROUTER_EXPERTS = 4, 5, 8


class Chain:

    def __init__(self, engine, semaphore):
        self.engine, self.semaphore, self.base, self.n = engine, semaphore, 0, 0

    def __call__(self, instruction):
        instruction.then_inc(self.semaphore, 1)
        self.n += 1

    def wait(self, alone=False):
        if isinstance(self.base, int) and self.base + self.n == 0:
            return
        if alone:
            wait_alone(self.engine, self.semaphore, self.base + self.n)
        else:
            self.engine.wait_ge(self.semaphore, self.base + self.n)


def run_steps(engine, step, chain=None, first=-2, last=B + 1, loop=LOOP, stride=1):
    for b in range(first, loop[0]):
        step(b)
    if chain is None:
        with engine.Fori(loop[0], loop[-1] + 1) as b:
            step(b)
    else:
        done, chain.n = chain.n, 0
        per = chain.per
        with engine.Fori(loop[0], loop[-1] + 1) as b:
            chain.base = b * per + (done - loop[0] * per)
            step(b)
            assert chain.n == per, (chain.n, per)
        chain.base, chain.n = 0, done + per * len(loop)
    for b in range(loop[-1] + 1, last):
        step(b)


def layer_kernel(nc, x, wqkv, bqkv, wproj, bproj, gate_w, w1, w2, w3, ws1, ws2, ws3, consts, out):
    with ExitStack() as ctx:
        def sb(name, shape, dt=F32):
            return ctx.enter_context(nc.sbuf_tensor(name, shape, dt))

        def dram(name, shape, dt):
            return nc.dram_tensor(name, shape, dt, kind="Internal").ap()

        w = {
            "identf": sb("identf", [P, P]),
            "w1h": sb("w1h", [P, (NCH + 1) * P], F32R), "w1l": sb("w1l", [P, (NCH + 1) * P], F32R),
            "w3h": sb("w3h", [P, (NCH + 1) * P], F32R), "w3l": sb("w3l", [P, (NCH + 1) * P], F32R),
            "w2h": sb("w2h", [P, (NCH + 1) * P], F32R), "w2l": sb("w2l", [P, (NCH + 1) * P], F32R),
            "selb": sb("selb", [SPLIT * NEXP, NCH, P], BF16), "identb": sb("identb", [P, P], BF16),
            "less": sb("less", [P, C_END - C_L16]),
            "x1t_d": dram("x1t_d", [B, P, T], F32),
            "e_d": dram("e_d", [B, P, TT * NEXP], F32),
        }
        attention_pass(nc, w, x, wqkv, bqkv, wproj, bproj, gate_w, w1, w2, w3, ws1, ws2, ws3, consts)
        expert_pass(nc, w, out)


def product(nc, dst, high, low, right_high, right_low, start=True, stop=True):
    nc.tensor.matmul(dst, high, right_high, start=start, stop=False)
    nc.tensor.matmul(dst, high, right_low, start=False, stop=False)
    return nc.tensor.matmul(dst, low, right_high, start=False, stop=stop)


def norm_seed(nc, chain, mv, small, done):
    y, t, var, half = (small[:, n, :] for n in range(4))
    chain(nc.vector.tensor_scalar(var, mv[:, :, 1], EPS, None, ALU.add))
    chain.wait()
    chain(nc.vector.tensor_scalar(t.bitcast(I32), var.bitcast(I32), 1, None, ALU.logical_shift_right))
    chain(nc.vector.tensor_scalar(half, var, -0.5, None, ALU.mult))
    chain.wait()
    nc.vector.tensor_scalar(y.bitcast(I32), t.bitcast(I32), -1.0, float(0x5F3759DF), ALU.mult, ALU.add).then_inc(done, 1)


def norm_newton(nc, chain, small):
    y, t, half = (small[:, n, :] for n in (0, 1, 3))
    chain(nc.gpsimd.tensor_tensor(t, y, y, ALU.mult))
    chain.wait()
    chain(nc.gpsimd.tensor_tensor(t, t, half, ALU.mult))
    chain.wait(alone=True)
    chain(nc.gpsimd.tensor_scalar(t, t, 1.5, None, ALU.add))
    chain.wait()
    chain(nc.gpsimd.tensor_tensor(y, y, t, ALU.mult))
    chain.wait()


def attention_pass(nc, w, x, wqkv, bqkv, wproj, bproj, gate_w, w1, w2, w3, ws1, ws2, ws3, consts):
    ctx = ExitStack()
    with ctx:
        def sb(name, shape, dt=F32):
            return ctx.enter_context(nc.sbuf_tensor(name, shape, dt))

        def sem(name):
            return ctx.enter_context(nc.semaphore(name))

        identf, identb = w["identf"], w["identb"]
        wraw = sb("wraw", [P, 3 * E])
        wrope = sb("wrope", [P, 4, P])
        wropeh = sb("wropeh", [P, 4, P], F32R)
        wropel = sb("wropel", [P, 4, P], F32R)
        brow = sb("brow", [1, 3 * E])
        brope = sb("brope", [1, 4, P])
        bprow = sb("bprow", [1, E])
        ones = sb("ones", [1, P])
        bcol = sb("bcol", [P, 4])
        bv = sb("bv", [P, E])
        bp = sb("bp", [P, E])
        wp = sb("wp", [P, E])
        gwrow = sb("gwrow", [NEXP, E])
        gwt = sb("gwt", [P, NEXP])
        cos = sb("cos", [P, T])
        sin = sb("sin", [P, T])
        maskf = sb("maskf", [P, P])
        maskb = sb("maskb", [P, P], BF16)
        self_ = sb("self_", [SPLIT * NEXP, NCH * P])
        wraw1 = sb("wraw1", [P, (NCH + 1) * P])
        wraw3 = sb("wraw3", [P, (NCH + 1) * P])
        wraw2 = sb("wraw2", [P, (NCH + 1) * P])
        EXPERT_WEIGHTS = ((wraw1, w["w1h"], w["w1l"]), (wraw3, w["w3h"], w["w3l"]), (wraw2, w["w2h"], w["w2l"]))
        x_in = sb("x_in", [P, TT, E])
        xt = sb("xt", [P, T])
        xth = sb("xth", [P, T], F32R)
        xtl = sb("xtl", [P, T], F32R)
        rope_cos = sb("rope_cos", [P, 2, T])
        rope_sin = sb("rope_sin", [P, 2, T])
        roped = sb("roped", [P, 2, T])
        rest = sb("rest", [P, 2, T])
        parts = sb("parts", [P, 2, SPLIT, T], BF16)
        qs = sb("qs", [P, G, HG * T], BF16)
        ks = sb("ks", [P, G, HG * T], BF16)
        vfresh = sb("vfresh", [P, TT, E])
        vstage = sb("vstage", [P, TT, E])
        v = sb("v", [P, G, TT, HG, 32])
        mx = sb("mx", [P, G, HG, TT])
        negm = sb("negm", [P, SPLIT, HG * TT], BF16)
        mrest = sb("mrest", [P, 2, HG * TT])
        mrows = sb("mrows", [SPLIT * HG * TT, P], BF16)
        probs = sb("probs", [P, 2, B_UNITS, 2 * T])
        ot = sb("ot", [P, T])
        rden = sb("rden", [P, TT, HG])
        o = sb("o", [P, TT, E])
        ot2 = sb("ot2", [P, T])
        xres = sb("xres", [P, TT, E])
        xb = sb("xb", [P, TT, E])
        r = sb("r", [P, TT, E])
        st = sb("st", [P, TT, 6])
        mv = sb("mv", [P, TT, 2])
        small = sb("small", [P, 4, TT])
        x1 = sb("x1", [P, TT, E])
        x1t = sb("x1t", [P, T])
        lmax = sb("lmax", [P, TT])
        z = sb("z", [P, TT, NEXP])
        ez = sb("ez", [P, TT * NEXP])

        bounce = nc.dram_tensor("bounce", [B, 2, NPROD, P, T], BF16, kind="Internal").ap()

        psA = [ctx.enter_context(nc.psum_tensor(f"psA{i}", [P, T], F32)) for i in range(2)]
        psB = [ctx.enter_context(nc.psum_tensor(f"psB{i}", [P, 2 * T], F32)) for i in range(2)]
        psO = ctx.enter_context(nc.psum_tensor("psO", [P, T], F32))
        psM = ctx.enter_context(nc.psum_tensor("psM", [P, T], F32))

        wqkv_in = sem("wqkv_in")
        consts_in = sem("consts_in")
        weights_in = sem("weights_in")
        weights_rounded = sem("weights_rounded")
        weights_low = sem("weights_low")
        selb_ready = sem("selb_ready")
        setup_dve = sem("setup_dve")
        setup_pe = sem("setup_pe")
        setup_pool = sem("setup_pool")
        x_in_loaded = sem("x_in_loaded")
        xres_loaded = sem("xres_loaded")
        parts_ready = sem("parts_ready")
        bounced = sem("bounced")
        qk_loaded = [sem(f"qk_loaded{g}") for g in range(G)]
        mrows_loaded = [sem(f"mrows_loaded{g}") for g in range(G)]
        a_scored = sem("a_scored")
        a_reduced = sem("a_reduced")
        negm_ready = sem("negm_ready")
        b_scored = sem("b_scored")
        exp_done = sem("exp_done")
        causal_done = sem("causal_done")
        pv_done = sem("pv_done")
        ot_copied = sem("ot_copied")
        v_moved = sem("v_moved")
        v_copied = sem("v_copied")
        xtl_ready = sem("xtl_ready")
        roped_ready = sem("roped_ready")
        part0_ready = sem("part0_ready")
        rest_ready = sem("rest_ready")
        part1_ready = sem("part1_ready")
        item_full = sem("item_full")
        item_free = sem("item_free")
        xb_ready = sem("xb_ready")
        x1_ready = sem("x1_ready")
        ez_ready = sem("ez_ready")
        x1t_stored = sem("x1t_stored")
        ez_stored = sem("ez_stored")
        seed_ready = sem("seed_ready")
        dve_own = sem("dve_own")
        pool_own = sem("pool_own")

        xv = x.rearrange("b (t p) e -> b p t e", p=P)

        block = ctx.enter_context(nc.Block())

        @block.sync
        def _(sp):
            for dst, src in (
                (wraw[:, :], wqkv), (brow[:, :], bqkv.rearrange("(a n) -> a n", a=1)), (identf[:, :], consts[:, C_ID:C_ID + P]),
            ):
                sp.dma_start(dst, src).then_inc(wqkv_in, 16)
            sp.dma_start(x_in[:, :, :], xv[0]).then_inc(x_in_loaded, 16)
            for dst, src in (
                (bprow[:, :], bproj.rearrange("(a n) -> a n", a=1)),
                (gwrow[:, :], gate_w), (cos[:, :], consts[:, C_COS:C_COS + T]), (sin[:, :], consts[:, C_SIN:C_SIN + T]),
                (maskf[:, :], consts[:, C_MASK:C_MASK + P]),
            ):
                sp.dma_start(dst, src).then_inc(consts_in, 16)
            for dst, src in (
                (wp[:, :], wproj), (self_[:, :], consts[0:SPLIT * NEXP, C_SEL:C_L16]),
                (w["less"][:, :], consts[:, C_L16:C_END]),
                (wraw1[:, 0:NEXP * INTER].rearrange("d (e i) -> d e i", e=NEXP), w1.rearrange("e d i -> d e i")),
                (wraw3[:, 0:NEXP * INTER].rearrange("d (e i) -> d e i", e=NEXP), w3.rearrange("e d i -> d e i")),
                (wraw2[:, 0:NCH * E].rearrange("p (c d) -> p c d", c=NCH),
                 w2.rearrange("e i d -> (e i) d").rearrange("(c p) d -> p c d", p=P)),
                (wraw1[:, NCH * P:], ws1), (wraw3[:, NCH * P:], ws3), (wraw2[:, NCH * P:], ws2),
            ):
                sp.dma_start(dst, src).then_inc(weights_in, 16)

            def load_group(b, g):
                wait_alone(sp, bounced, 96 * (b + 1))
                if exists(b, -1):
                    wait_alone(sp, b_scored, B_UNITS * G * (b - 1) + B_UNITS * (g + 1))
                for side, dst in ((0, qs), (1, ks)):
                    sp.dma_start(dst[0:KROWS, g, :],
                                 bounce[b, side][:, 32 * g:32 * g + 32, :].rearrange("a (d h) t -> a d (h t)", h=HG)
                                 ).then_inc(qk_loaded[g], 16)

            def load_mrows(b, g, body, item):
                wait_alone(sp, item_free, item_no(body, item))
                sp.dma_start(qs[MROW:MROW + SPLIT, g, :], mrows[:, :]).then_inc(mrows_loaded[g], 16)

            def bounce_parts(b, side):
                wait_alone(sp, parts_ready, 2 * b + side + 1)
                for n in range(SPLIT):
                    rows = bounce[b, 0][n::SPLIT] if side == 0 else bounce[b, 1][SPLIT * n:SPLIT * n + SPLIT]
                    sp.dma_start(rows.rearrange("i p t -> p i t"), parts[:, side, :, :]).then_inc(bounced, 16)

            def step(b):
                if exists(b, 0):
                    load_group(b, 3)
                    load_mrows(b, 1, b, "m1")
                if exists(b, -1):
                    if exists(b, -2):
                        wait_alone(sp, xb_ready, b - 1)
                    sp.dma_start(xres[:, :, :], xv[b - 1]).then_inc(xres_loaded, 16)
                if exists(b, 1):
                    load_group(b + 1, 0)
                if exists(b, 0):
                    load_mrows(b, 2, b, "m2")
                if exists(b, 3):
                    wait_alone(sp, item_full, item_no(b, "xt"))
                    sp.dma_start(x_in[:, :, :], xv[b + 3]).then_inc(x_in_loaded, 16)
                if exists(b, 2):
                    bounce_parts(b + 2, 0)
                if exists(b, 1):
                    load_group(b + 1, 1)
                if exists(b, 0):
                    load_mrows(b, 3, b, "m3")
                if exists(b, 2):
                    bounce_parts(b + 2, 1)
                if exists(b, 1):
                    load_group(b + 1, 2)
                    load_mrows(b + 1, 0, b, "m0")
                if exists(b, -1):
                    wait_alone(sp, item_free, item_no(b, "td"))
                    sp.dma_start(w["x1t_d"][b - 1], x1t[:, :]).then_inc(x1t_stored, 16)
                    wait_alone(sp, ez_ready, b)
                    sp.dma_start(w["e_d"][b - 1], ez[:, :]).then_inc(ez_stored, 16)

            run_steps(sp, step)
            sp.wait_ge(x1t_stored, 16 * B)
            sp.wait_ge(ez_stored, 16 * B)

        @block.gpsimd
        def _(pool):
            nc.gpsimd.memset(ks[:, :, :].bitcast(F32), 0.0).then_inc(setup_pool, 1)
            pool.wait_ge(setup_pool, 1)
            nc.gpsimd.memset(ks[MROW:MROW + SPLIT, :, :].bitcast(F32), BF16_ONES).then_inc(setup_pool, 1)
            pool.wait_ge(setup_pool, 2)

            def split(part, b, side):
                n = 2 * (b + 2) + side
                if part == 0:
                    pool.wait_ge(item_free, item_no(b, ("qr", "kr")[side]))
                    nc.gpsimd.tensor_tensor(roped[:, side, :], rope_cos[:, side, :], rope_sin[:, side, :],
                                            ALU.add).then_inc(roped_ready, 1)
                elif part == 1:
                    pool.wait_ge(part0_ready, n + 1)
                    nc.gpsimd.tensor_tensor(rest[:, side, :], roped[:, side, :], parts[:, side, 0, :],
                                            ALU.subtract).then_inc(rest_ready, 1)
                else:
                    pool.wait_ge(part1_ready, n + 1)
                    nc.gpsimd.tensor_tensor(parts[:, side, 2, :], rest[:, side, :], parts[:, side, 1, :],
                                            ALU.subtract).then_inc(parts_ready, 1)

            chain = Chain(pool, pool_own)
            chain.per = 4 * NEWTON

            def causal(ap, heads):
                return nc.gpsimd.affine_select(out=ap, in_=ap, compare_op=ALU.is_ge, fill=0.0, base=0,
                                               pattern=[[0, heads], [1, P]], channel_multiplier=-1)

            def step(b):
                for t in range(G):
                    for u in range(B_UNITS):
                        if (t, u) == (0, 1) and exists(b, 2):
                            pool.wait_ge(item_free, item_no(b, "xt"))
                            nc.gpsimd.tensor_tensor(xtl[:, :], xt[:, :], xth[:, :].bitcast(F32),
                                                    ALU.subtract).then_inc(xtl_ready, 1)
                        if (t, u) == (2, 4) and exists(b, -1):
                            pool.wait_ge(seed_ready, b)
                            for _ in range(NEWTON):
                                norm_newton(nc, chain, small)
                        if exists(b, 0):
                            wait_alone(pool, exp_done, B_UNITS * G * b + B_UNITS * t + u + 1)
                            unit = probs[:, t % 2, u, :]
                            if u < HG:
                                causal(unit.rearrange("p (a n) -> p a n", n=T)[:, :, 0:P], 2)
                                causal(unit[:, T + 384:2 * T].rearrange("p (a n) -> p a n", a=1), 1).then_inc(causal_done, 1)
                            else:
                                causal(unit.rearrange("p (a n) -> p a n", a=HG)[:, :, 0:P], HG).then_inc(causal_done, 1)
                        if isinstance(b, int) and b == -1 and t == 0 and u < len(EXPERT_WEIGHTS):
                            raw, high, low = EXPERT_WEIGHTS[u]
                            pool.wait_ge(weights_rounded, u + 1)
                            nc.gpsimd.tensor_tensor(low[:, :], raw[:, :], high[:, :].bitcast(F32),
                                                    ALU.subtract).then_inc(weights_low, 1)
                        for side, first in ((0, 4), (1, 9)):
                            if exists(b, 2) and B_UNITS * t + u - first in (0, 2, 4):
                                split((B_UNITS * t + u - first) // 2, b, side)
                        if (t, u) == (1, 1) and exists(b, -1):
                            pool.wait_ge(xres_loaded, 16 * b)
                            if exists(b, -2):
                                pool.wait_ge(item_free, item_no(b - 1, "tc"))
                            nc.gpsimd.tensor_tensor(xb[:, :, :], xres[:, :, :],
                                                    bp[:, :].rearrange("p (a n) -> p a n", a=1).broadcast_to([P, TT, E]),
                                                    ALU.add).then_inc(xb_ready, 1)

            pool.wait_ge(setup_dve, SETUP_DVE)
            run_steps(pool, step, chain)

        @block.scalar
        def _(act):
            def round_part(part, b, side):
                n = 2 * (b + 2) + side
                if part == 0:
                    act.wait_ge(roped_ready, n + 1)
                    if exists(b, 1):
                        act.wait_ge(bounced, 96 * (b + 2))
                    nc.scalar.copy(parts[:, side, 0, :], roped[:, side, :]).then_inc(part0_ready, 1)
                else:
                    act.wait_ge(rest_ready, n + 1)
                    nc.scalar.copy(parts[:, side, 1, :], rest[:, side, :]).then_inc(part1_ready, 1)

            def copy_v(b, g):
                act.wait_ge(v_moved, b + 1)
                if exists(b, -1):
                    act.wait_ge(pv_done, 4 * b - 4 + g + 1)
                nc.scalar.copy(v[:, g, :, :, 0:D],
                               vstage[:, :, 32 * g:32 * g + 32].rearrange("p t (h d) -> p t h d", d=D)
                               ).then_inc(v_copied, 1)

            def step(b):
                for t in range(G):
                    for u in range(B_UNITS):
                        if exists(b, 0):
                            n = B_UNITS * G * b + B_UNITS * t + u
                            act.wait_ge(b_scored, n + 1)
                            if t >= 2:
                                act.wait_ge(pv_done, 4 * b + t - 1)
                            elif exists(b, -1):
                                act.wait_ge(pv_done, 4 * b + t - 1)
                            nc.scalar.activation(probs[:, t % 2, u, :], psB[(B_UNITS * t + u) % 2][:, :], ACT.Exp,
                                                 scale=SCALE).then_inc(exp_done, 1)
                        if isinstance(b, int) and b == -1 and t == 0 and u < len(EXPERT_WEIGHTS):
                            act.wait_ge(weights_in, 16 * 9)
                            raw, high, _ = EXPERT_WEIGHTS[u]
                            nc.scalar.copy(high[:, :], raw[:, :]).then_inc(weights_rounded, 1)
                            if u == 0:
                                nc.scalar.copy(w["selb"][:, :, :].rearrange("p c n -> p (c n)"),
                                               self_[:, :]).then_inc(selb_ready, 1)
                        if u == 3 and exists(b, 0 if t else -1):
                            act.wait_ge(pv_done, 4 * b + t)
                            before = (b, ("ta3", "ta0", "ta1")[t - 1]) if t else (b - 1, "ta2")
                            if exists(before[0], SHIFT[before[1]]):
                                act.wait_ge(item_full, item_no(*before))
                            nc.scalar.copy(ot[:, :], psO[:, :]).then_inc(ot_copied, 1)
                        if (t, u) == (3, 4) and exists(b, -1):
                            act.wait_ge(item_free, item_no(b, "te"))
                            if exists(b, -2):
                                act.wait_ge(ez_stored, 16 * (b - 1))
                            nc.scalar.activation(ez[:, :], z[:, :, :].rearrange("p t e -> p (t e)"), ACT.Exp).then_inc(ez_ready, 1)
                        item = AT.get((t, u))
                        if item in ("tb", "xt", "td") and exists(b, SHIFT[item]):
                            act.wait_ge(item_full, item_no(b, item))
                            if item == "td" and exists(b, -2):
                                act.wait_ge(x1t_stored, 16 * (b - 1))
                            if item == "xt":
                                nc.scalar.copy(xth[:, :], psM[:, :])
                            dst = {"tb": ot2, "xt": xt, "td": x1t}[item]
                            nc.scalar.copy(dst[:, :], psM[:, :]).then_inc(item_free, 1)
                        for side, first in ((0, 5), (1, 10)):
                            if exists(b, 2) and B_UNITS * t + u - first in (0, 2):
                                round_part((B_UNITS * t + u - first) // 2, b, side)
                        for at, ahead, g in (((0, 1), 0, 2), ((1, 0), 0, 3), ((2, 1), 1, 0), ((3, 1), 1, 1)):
                            if (t, u) == at and exists(b, ahead):
                                copy_v(b + ahead, g)
                        if (t, u) == (1, 1) and exists(b, 1):
                            act.wait_ge(item_free, item_no(b - 1, "v"))
                            if exists(b, 0):
                                act.wait_ge(v_copied, 4 * b + 4)
                            nc.scalar.copy(vstage[:, :, :], vfresh[:, :, :]).then_inc(v_moved, 1)

            act.wait_ge(setup_dve, 3)
            run_steps(act, step)

        @block.tensor
        def _(pe):
            pe.wait_ge(setup_dve, SETUP_BIAS)
            pe.wait_ge(consts_in, 16 * 5)
            for i in range(4):
                nc.tensor.matmul(psM[:, i:i + 1], brope[0:1, i, :], ones[0:1, 0:1], start=True, stop=True)
            nc.tensor.matmul(psM[:, 8:8 + E], ones[0:1, :], brow[0:1, 2 * E:3 * E], start=True, stop=True)
            nc.tensor.matmul(psM[:, 136:136 + E], ones[0:1, :], bprow[0:1, :], start=True, stop=True)
            nc.tensor.transpose(psM[:, 264:264 + NEXP], gwrow[:, :], identf[0:NEXP, 0:NEXP]).then_inc(setup_pe, 1)
            pe.wait_ge(setup_dve, SETUP_DVE)
            pe.wait_ge(setup_pool, 2)

            def item(b, name):
                no = item_no(b, name)
                if not (isinstance(no, int) and no == 1):
                    wait_alone(pe, item_free, no - 1)
                if name in ("m0", "m1", "m2", "m3"):
                    g = int(name[1])
                    wait_alone(pe, negm_ready, 4 * (b + (g == 0)) + g + 1)
                    last = nc.tensor.transpose(psM[:, :].bitcast(BF16)[0:SPLIT * HG * TT, 0:P],
                                               negm[:, :, :].rearrange("p s n -> p (s n)"), identb[:, :])
                elif name == "xt":
                    pe.wait_ge(x_in_loaded, 16 * (b + 3))
                    for t in range(TT):
                        last = nc.tensor.transpose(psM[:, P * t:P * t + P], x_in[:, t, :], identf[:, :])
                elif name == "v":
                    for t in range(TT):
                        last = nc.tensor.matmul(psM[:, P * t:P * t + P], xt[:, P * t:P * t + P], wraw[:, 2 * E:3 * E],
                                                start=True, stop=True)
                elif name in ("q", "qr", "k", "kr"):
                    i = ("q", "qr", "k", "kr").index(name)
                    if name == "q":
                        pe.wait_ge(xtl_ready, b + 3)
                    last = product(nc, psM[:, :], wropeh[:, i, :], wropel[:, i, :], xth[:, :], xtl[:, :])
                elif name[:2] == "ta":
                    g = int(name[2])
                    pe.wait_ge(ot_copied, 4 * (b + SHIFT[name]) + g + 1)
                    for t in range(TT):
                        last = nc.tensor.transpose(psM[:, P * t:P * t + P], ot[:, P * t:P * t + P], identf[:, :])
                elif name == "tb":
                    for t in range(TT):
                        last = nc.tensor.transpose(psM[:, P * t:P * t + P], o[:, t, :], identf[:, :])
                elif name == "tc":
                    pe.wait_ge(weights_in, 16 * 9)
                    for t in range(TT):
                        last = nc.tensor.matmul(psM[:, P * t:P * t + P], ot2[:, P * t:P * t + P], wp[:, :],
                                                start=True, stop=True)
                elif name == "td":
                    pe.wait_ge(x1_ready, b)
                    for t in range(TT):
                        last = nc.tensor.transpose(psM[:, P * t:P * t + P], x1[:, t, :], identf[:, :])
                elif name == "te":
                    for t in range(TT):
                        last = nc.tensor.matmul(psM[:, NEXP * t:NEXP * t + NEXP], x1t[:, P * t:P * t + P], gwt[:, :],
                                                start=True, stop=True)
                last.then_inc(item_full, 1)

            def score_a(b, g, unit):
                if unit < 8:
                    qt, heads = (3, [unit]) if unit < 4 else (2, [unit - 4])
                else:
                    qt, heads = (1, [2 * unit - 16, 2 * unit - 15]) if unit < 10 else (0, range(HG))
                if unit == 0:
                    pe.wait_ge(qk_loaded[g], 32 * (b + 1))
                n = A_UNITS * G * b + A_UNITS * g + unit
                if not (isinstance(n, int) and n < 2):
                    pe.wait_ge(a_reduced, n - 1)
                bank, width = psA[(A_UNITS * g + unit) % 2], P * (qt + 1)
                for i, h in enumerate(heads):
                    nc.tensor.matmul(bank[:, width * i:width * i + width],
                                     qs[0:KA, g, T * h + P * qt:T * h + P * qt + P], ks[0:KA, g, T * h:T * h + width],
                                     start=True, stop=False)
                    last = nc.tensor.matmul(bank[:, width * i + width - P:width * i + width], identb[:, :], maskb[:, :],
                                            start=False, stop=True)
                last.then_inc(a_scored, 1)

            def score_b(b, g, u):
                n = B_UNITS * G * b + B_UNITS * g + u
                if u == 0:
                    pe.wait_ge(mrows_loaded[g], 16 * (b + 1))
                if not (isinstance(n, int) and n < 2):
                    pe.wait_ge(exp_done, n - 1)
                dst = psB[(B_UNITS * g + u) % 2]
                if u < HG:
                    todo = [(T * u, 0, 0), (T * u, 1, T), (T * u, 3, T + 384)]
                else:
                    todo = [(T * h, 2, 256 * h) for h in range(HG)]
                for at, kt, col in todo:
                    last = nc.tensor.matmul(dst[:, col:col + T - P * kt], ks[:, g, at + P * kt:at + P * kt + P],
                                            qs[:, g, at + P * kt:at + T], start=True, stop=True)
                last.then_inc(b_scored, 1)

            def weigh(b, g, part):
                kt = (0, 1, 3, 2)[part]
                if part == 0:
                    if not (isinstance(b, int) and 4 * b + g < 1):
                        pe.wait_ge(ot_copied, 4 * b + g)
                    pe.wait_ge(v_copied, 4 * b + g + 1)
                for h in range(HG):
                    if part == 0:
                        pe.wait_ge(causal_done, B_UNITS * G * b + B_UNITS * g + h + 1)
                    if part == 3 and h == 0:
                        pe.wait_ge(causal_done, B_UNITS * G * b + B_UNITS * (g + 1))
                    unit, at = (h, (0, T, 0, T + 384)[kt]) if kt != 2 else (HG, 256 * h)
                    last = nc.tensor.matmul(psO[32 * h:32 * h + 32, P * kt:T], v[:, g, kt, h, :],
                                            probs[:, g % 2, unit, at:at + T - P * kt],
                                            start=(part == 0), stop=(part == 3))
                if part == 3:
                    last.then_inc(pv_done, 1)

            def step(b):
                for t in range(G):
                    for u in range(B_UNITS):
                        if exists(b, 0):
                            score_b(b, t, u)
                        ahead, ga = (0, t + 2) if t < 2 else (1, t - 2)
                        name = AT.get((t, u))
                        units = range(*A_SPLIT[u]) if exists(b, ahead) else ()
                        for unit in units[:1]:
                            score_a(b + ahead, ga, unit)
                        if u == 4 and name and exists(b, SHIFT[name]):
                            item(b, name)
                        back, gp = (0, t - 1) if t else (-1, 3)
                        if u < 4 and exists(b, back):
                            weigh(b + back, gp, u)
                        for unit in units[1:]:
                            score_a(b + ahead, ga, unit)
                        if u < 4 and name and exists(b, SHIFT[name]):
                            item(b, name)

            run_steps(pe, step)

        @block.vector
        def _(dve):
            chain = Chain(dve, dve_own)
            chain.per = 4 * 3 + 4 + 1 + 2 * TT + 3
            nc.vector.memset(qs[:, :, :].bitcast(F32), 0.0).then_inc(setup_dve, 1)
            nc.vector.memset(v[:, :, :, :, :], 0.0).then_inc(setup_dve, 1)
            dve.wait_ge(setup_dve, 2)
            nc.vector.memset(v[:, :, :, :, D:D + 1], 1.0).then_inc(setup_dve, 1)
            dve.wait_ge(wqkv_in, 16 * 3)
            nc.vector.tensor_copy(identb[:, :], identf[:, :]).then_inc(setup_dve, 1)
            nc.vector.memset(ones[:, :], 1.0).then_inc(setup_dve, 1)

            def spread(dst, src):
                plain = dst[:, 0, :].rearrange("p (g d h) -> p g h d", g=G, d=D)
                turned = dst[:, 1, :].rearrange("p (g d two h) -> p g h d two", g=G, d=D // 2, two=2)
                given = src.rearrange("p (g h d) -> p g h d", g=G, h=HG)
                pairs = src.rearrange("p (g h d two) -> p g h d two", g=G, h=HG, two=2)
                nc.vector.tensor_copy(plain, given)
                nc.vector.tensor_scalar(turned[:, :, :, :, 0], pairs[:, :, :, :, 1], -1.0, None, ALU.mult)
                last = nc.vector.tensor_copy(turned[:, :, :, :, 1], pairs[:, :, :, :, 0])
                last.then_inc(setup_dve, 1)

            for side in range(2):
                spread(wrope[:, 2 * side:2 * side + 2, :], wraw[:, E * side:E * side + E])
                spread(brope[:, 2 * side:2 * side + 2, :], brow[:, E * side:E * side + E])
            dve.wait_ge(consts_in, 16 * 5)
            nc.vector.tensor_copy(maskb[:, :], maskf[:, :]).then_inc(setup_dve, 1)
            nc.vector.memset(st[:, :, :], 0.0).then_inc(setup_dve, 1)
            dve.wait_ge(setup_dve, SETUP_BIAS)
            nc.vector.tensor_copy(wropeh[:, :, :], wrope[:, :, :]).then_inc(setup_dve, 1)
            dve.wait_ge(setup_dve, SETUP_BIAS + 1)
            nc.vector.tensor_tensor(wropel[:, :, :], wrope[:, :, :], wropeh[:, :, :].bitcast(F32),
                                    ALU.subtract).then_inc(setup_dve, 1)
            dve.wait_ge(setup_pe, 1)
            nc.vector.tensor_copy(bcol[:, :], psM[:, 0:4]).then_inc(setup_dve, 1)
            nc.vector.tensor_copy(bv[:, :], psM[:, 8:8 + E]).then_inc(setup_dve, 1)
            nc.vector.tensor_copy(bp[:, :], psM[:, 136:136 + E]).then_inc(setup_dve, 1)
            nc.vector.tensor_copy(gwt[:, :], psM[:, 264:264 + NEXP]).then_inc(setup_dve, 1)
            nc.vector.memset(small[:, :, :], 0.0).then_inc(setup_dve, 1)
            nc.vector.memset(mv[:, :, :], 0.0).then_inc(setup_dve, 1)
            dve.wait_ge(setup_dve, SETUP_DVE)

            def reduce_a(b, g, unit):
                dve.wait_ge(a_scored, A_UNITS * G * b + A_UNITS * g + unit + 1)
                bank = psA[(A_UNITS * g + unit) % 2]
                if unit < 8:
                    qt, h0, n = (3, unit, 1) if unit < 4 else (2, unit - 4, 1)
                else:
                    qt, h0, n = (1, 2 * unit - 16, 2) if unit < 10 else (0, 0, HG)
                width = P * (qt + 1)
                nc.vector.tensor_reduce(mx[:, g, h0:h0 + n, qt],
                                        bank[:, 0:width * n].rearrange("p (a n) -> p a n", a=n),
                                        AX_X, ALU.max).then_inc(a_reduced, 1)

            def split_max(b, g):
                dve.wait_ge(a_reduced, A_UNITS * G * b + A_UNITS * (g + 1))
                m = mx[:, g, :, :].rearrange("p h t -> p (h t)")
                chain(nc.vector.tensor_scalar(negm[:, 0, :], m, -1.0, None, ALU.mult))
                chain.wait()
                chain(nc.vector.scalar_tensor_tensor(out=mrest[:, 0, :], in0=m, scalar=-1.0, in1=negm[:, 0, :],
                                                     op0=ALU.mult, op1=ALU.subtract))
                chain.wait()
                chain(nc.vector.tensor_copy(negm[:, 1, :], mrest[:, 0, :]))
                chain.wait()
                nc.vector.tensor_tensor(negm[:, 2, :], mrest[:, 0, :], negm[:, 1, :], ALU.subtract).then_inc(negm_ready, 1)

            def item(b, name):
                dve.wait_ge(item_full, item_no(b, name))
                if name in ("m0", "m1", "m2", "m3"):
                    g = int(name[1])
                    if g:
                        dve.wait_ge(mrows_loaded[g - 1], 16 * (b + 1))
                    elif exists(b, 0):
                        dve.wait_ge(mrows_loaded[3], 16 * (b + 1))
                    nc.vector.tensor_copy(mrows[:, :], psM[:, :].bitcast(BF16)[0:SPLIT * HG * TT, 0:P]).then_inc(item_free, 1)
                elif name == "v":
                    if exists(b, 1):
                        dve.wait_ge(v_moved, b + 2)
                    nc.vector.tensor_tensor(vfresh[:, :, :], psM[:, :].rearrange("p (t e) -> p t e", t=TT),
                                            bv[:, :].rearrange("p (a n) -> p a n", a=1).broadcast_to([P, TT, E]),
                                            ALU.add).then_inc(item_free, 1)
                elif name in ("q", "qr", "k", "kr"):
                    side, turned = name[0] == "k", len(name) == 2
                    if not turned and exists(b, 1):
                        dve.wait_ge(roped_ready, 2 * (b + 2) - 1 + side)
                    dst, table = (rope_sin, sin) if turned else (rope_cos, cos)
                    nc.vector.scalar_tensor_tensor(out=dst[:, int(side), :], in0=psM[:, :],
                                                   scalar=bcol[:, 2 * side + turned:2 * side + turned + 1],
                                                   in1=table[:, :], op0=ALU.add, op1=ALU.mult).then_inc(item_free, 1)
                elif name[:2] == "ta":
                    g = int(name[2])
                    got = psM[:, :].rearrange("p (t h c) -> p t h c", t=TT, h=HG)
                    chain(nc.vector.reciprocal(rden[:, :, :], got[:, :, :, D]))
                    chain.wait()
                    nc.vector.tensor_tensor(o[:, :, 32 * g:32 * g + 32].rearrange("p t (h d) -> p t h d", h=HG),
                                            got[:, :, :, 0:D],
                                            rden[:, :, :].rearrange("p t (h a) -> p t h a", a=1).broadcast_to([P, TT, HG, D]),
                                            ALU.mult).then_inc(item_free, 1)
                elif name == "tc":
                    dve.wait_ge(xb_ready, b)
                    nc.vector.tensor_tensor(r[:, :, :], psM[:, :].rearrange("p (t e) -> p t e", t=TT), xb[:, :, :],
                                            ALU.add).then_inc(item_free, 1)
                elif name == "te":
                    logits = psM[:, 0:TT * NEXP].rearrange("p (t e) -> p t e", t=TT)
                    chain(nc.vector.tensor_reduce(lmax[:, :], logits, AX_X, ALU.max))
                    chain.wait()
                    if exists(b, -2):
                        dve.wait_ge(ez_ready, b - 1)
                    nc.vector.tensor_tensor(z[:, :, :], logits,
                                            lmax[:, :].rearrange("p (t a) -> p t a", a=1).broadcast_to([P, TT, NEXP]),
                                            ALU.subtract).then_inc(item_free, 1)

            def step(b):
                for t in range(G):
                    for u in range(B_UNITS):
                        ahead, ga = (0, t + 2) if t < 2 else (1, t - 2)
                        units = range(*A_SPLIT[u]) if exists(b, ahead) else ()
                        early = (t, u) == (3, 2)
                        for unit in units[:1] if not early else ():
                            reduce_a(b + ahead, ga, unit)
                        ahead_m, gm = (0, t + 1) if t < 3 else (1, 0)
                        if u == 0 and exists(b, ahead_m):
                            split_max(b + ahead_m, gm)
                        if exists(b, -1):
                            if (t, u) == (2, 1):
                                dve.wait_ge(item_free, item_no(b, "tc"))
                                for n in range(TT):
                                    chain(nc.vector.bn_stats(st[:, n, :], r[:, n, :]))
                            if (t, u) == (2, 2):
                                chain.wait(alone=True)
                                for n in range(TT):
                                    chain(nc.vector.bn_aggr(mv[:, n, :], st[:, n, :]))
                            if (t, u) == (2, 3):
                                chain.wait()
                                norm_seed(nc, chain, mv, small, seed_ready)
                            if (t, u) in ((3, 1), (3, 2)):
                                if u == 1:
                                    dve.wait_ge(pool_own, 4 * NEWTON * b)
                                    if exists(b, -2):
                                        dve.wait_ge(item_full, item_no(b - 1, "td"))
                                for n in (2 * u - 2, 2 * u - 1):
                                    last = nc.vector.tensor_scalar(x1[:, n, :], r[:, n, :], mv[:, n, 0:1],
                                                                   small[:, 0, n:n + 1], ALU.subtract, ALU.mult)
                                if u == 2:
                                    last.then_inc(x1_ready, 1)
                        for unit in units[1:] if not early else units:
                            reduce_a(b + ahead, ga, unit)
                        name = AT.get((t, u))
                        if name and name not in ("tb", "xt", "td") and exists(b, SHIFT[name]):
                            item(b, name)

            run_steps(dve, step, chain)


def expert_pass(nc, w, out):
    NC1 = NCH + 1
    LAG = 3
    A_BUFS, PART_BUFS = 3, 6
    assert 2 * NC1 % PART_BUFS == 0
    ctx = ExitStack()
    with ctx:
        def sb(name, shape, dt=F32):
            return ctx.enter_context(nc.sbuf_tensor(name, shape, dt))

        def sem(name):
            return ctx.enter_context(nc.semaphore(name))

        identf, identb = w["identf"], w["identb"]
        less16 = w["less"][:, 0:NEXP * NEXP].rearrange("p (e f) -> p e f", e=NEXP)
        less4 = w["less"][:, NEXP * NEXP:].rearrange("p (e f) -> p e f", e=NGRP)

        x1t = [sb(f"x1t_{i}", [P, T]) for i in range(2)]
        xh = [sb(f"xh_{i}", [P, T], F32R) for i in range(2)]
        xl = [sb(f"xl_{i}", [P, T], F32R) for i in range(2)]
        ez = sb("ez2", [P, TT, NEXP])
        ct = [sb(f"ct_{i}", [SPLIT * NEXP, T], BF16) for i in range(2)]
        esum = sb("esum", [P, TT])
        erec = sb("erec", [P, TT])
        scores = [sb(f"score_{i}", [P, TT, NEXP]) for i in range(2)]
        gmax = sb("gmax", [P, TT, NGRP])
        gd = sb("gd", [P, TT, NGRP, NGRP])
        ge = sb("ge", [P, TT, NGRP, NGRP])
        grank = sb("grank", [P, TT, NGRP])
        masked = sb("masked", [P, TT, NEXP])
        ed = sb("ed", [P, TT, NEXP, NEXP])
        ee = sb("ee", [P, TT, NEXP, NEXP])
        erank = sb("erank", [P, TT, NEXP])
        c = sb("c", [P, TT, NEXP])
        crest = sb("crest", [P, TT, NEXP])
        cparts = sb("cparts", [P, TT, SPLIT, NEXP], BF16)
        s = [sb(f"s_{i}", [P, T]) for i in range(2)]
        sh = [sb(f"sh_{i}", [P, T]) for i in range(2)]
        a = [sb(f"a_{i}", [P, T]) for i in range(A_BUFS)]
        ah = [sb(f"ah_{i}", [P, T], F32R) for i in range(PART_BUFS)]
        al = [sb(f"al_{i}", [P, T], F32R) for i in range(PART_BUFS)]
        yt = sb("yt", [P, T])
        st = sb("st2", [P, TT, 6])
        mv = sb("mv2", [P, TT, 2])
        small = sb("small2", [P, 4, TT])
        res = sb("res", [P, TT, E])

        psH1 = [ctx.enter_context(nc.psum_tensor(f"psH1_{i}", [P, T], F32)) for i in range(2)]
        psH3 = [ctx.enter_context(nc.psum_tensor(f"psH3_{i}", [P, T], F32)) for i in range(2)]
        psC = [ctx.enter_context(nc.psum_tensor(f"psC_{i}", [P, T], F32)) for i in range(2)]
        psY = ctx.enter_context(nc.psum_tensor("psY", [P, T], F32))
        psM = ctx.enter_context(nc.psum_tensor("psM2", [P, T], F32))

        x1t_loaded = [sem(f"x1t_loaded{i}") for i in range(2)]
        ez_loaded = sem("ez_loaded")
        xh_ready = sem("xh_ready")
        xl_ready = sem("xl_ready")
        masked_ready = sem("masked_ready")
        ed_ready = sem("ed_ready")
        cparts_ready = sem("cparts_ready")
        ct_transposed = sem("ct_transposed")
        ct_copied = sem("ct_copied")
        h1_ready = sem("h1_ready")
        hc_ready = sem("hc_ready")
        silu_ready = sem("silu_ready")
        a_ready = sem("a_ready")
        ah_ready = sem("ah_ready")
        al_ready = sem("al_ready")
        y_added = sem("y_added")
        yt_ready = sem("yt_ready")
        y_turned = sem("y_turned")
        sh_ready = sem("sh_ready")
        scales_ready = sem("scales_ready")
        res_ready = sem("res_ready")
        out_stored = sem("out_stored")
        router_own = sem("router_own")
        norm_own = sem("norm_own")

        ov = out.rearrange("b (t p) e -> b p t e", p=P)
        block = ctx.enter_context(nc.Block())

        def run_pairs(engine, step, *chains):
            step(0, 0)
            step(1, 1)
            done = [chain.n for chain in chains]
            with engine.Fori(1, B // 2 - 1) as i:
                for chain, before in zip(chains, done):
                    chain.base, chain.n = i * (2 * chain.per) + (before - 2 * chain.per), 0
                for par in range(2):
                    step(i * 2 + par, par)
            for chain, before in zip(chains, done):
                assert chain.n == 2 * chain.per, chain.n
                chain.base, chain.n = 0, before + 2 * chain.per * (B // 2 - 2)
            step(B - 2, 0)
            step(B - 1, 1)

        def first(b):
            return isinstance(b, int) and b == 0

        def follows(b, n):
            return not isinstance(b, int) or b + n < B

        def from_chunk(n, start):
            return not isinstance(n, int) or n >= start

        def nth(par, ch):
            return NC1 * par + ch

        @block.sync
        def _(sp):
            def load_logits(b):
                if not first(b):
                    wait_alone(sp, masked_ready, b)
                sp.dma_start(ez[:, :, :], w["e_d"][b].rearrange("p (t e) -> p t e", t=TT)).then_inc(ez_loaded, 16)

            def load_x(b, par):
                if from_chunk(b, 2):
                    wait_alone(sp, yt_ready, b - 1)
                sp.dma_start(x1t[par][:, :], w["x1t_d"][b]).then_inc(x1t_loaded[par], 16)

            def step(b, par):
                if follows(b, 2):
                    load_logits(b + 2)
                if follows(b, 1) and not first(b):
                    load_x(b + 1, 1 - par)
                if from_chunk(b, 2):
                    wait_alone(sp, res_ready, b - 1)
                    sp.dma_start(ov[b - 2], res[:, :, :]).then_inc(out_stored, 16)

            load_logits(0)
            load_x(0, 0)
            load_x(1, 1)
            load_logits(1)
            run_pairs(sp, step)
            for b in (B - 2, B - 1):
                sp.wait_ge(res_ready, b + 1)
                sp.dma_start(ov[b], res[:, :, :]).then_inc(out_stored, 16)
            sp.wait_ge(out_stored, 16 * B)

        @block.gpsimd
        def _(pool):
            def low_x(b, par):
                pool.wait_ge(xh_ready, b + 1)
                nc.gpsimd.tensor_tensor(xl[par][:, :], x1t[par][:, :], xh[par][:, :].bitcast(F32),
                                        ALU.subtract).then_inc(xl_ready, 1)

            def expert_differences(b):
                pool.wait_ge(masked_ready, b + 1)
                nc.gpsimd.tensor_tensor(
                    ed[:, :, :, :], masked[:, :, :].rearrange("p t (a f) -> p t a f", a=1).broadcast_to([P, TT, NEXP, NEXP]),
                    masked[:, :, :].rearrange("p t (e a) -> p t e a", a=1).broadcast_to([P, TT, NEXP, NEXP]),
                    ALU.subtract).then_inc(ed_ready, 1)

            def step(b, par):
                for ch in range(NC1):
                    n, k = NC1 * b + ch, nth(par, ch)
                    if ch == NCH and follows(b, 2):
                        expert_differences(b + 2)
                    pool.wait_ge(ah_ready, n + 1)
                    nc.gpsimd.tensor_tensor(al[k % PART_BUFS][:, :], a[k % A_BUFS][:, :],
                                            ah[k % PART_BUFS][:, :].bitcast(F32),
                                            ALU.subtract).then_inc(al_ready, 1)
                    if ch == 5 and follows(b, 1):
                        low_x(b + 1, 1 - par)

            low_x(0, 0)
            expert_differences(0)
            expert_differences(1)
            run_pairs(pool, step)

        @block.scalar
        def _(act):
            def high_x(b, par):
                act.wait_ge(x1t_loaded[par], (b - par) * 8 + 16)
                if not (isinstance(b, int) and b < 2):
                    act.wait_ge(hc_ready, NC1 * (b - 1))
                nc.scalar.copy(xh[par][:, :], x1t[par][:, :]).then_inc(xh_ready, 1)

            def copy_ct(b, par):
                act.wait_ge(ct_transposed, b + 1)
                nc.scalar.copy(ct[par][:, :], psC[1 - par][:, :].bitcast(BF16)[0:SPLIT * NEXP, 0:T]).then_inc(ct_copied, 1)

            def normalise(b, half):
                if half == 0:
                    act.wait_ge(scales_ready, b + 1)
                    if not first(b):
                        act.wait_ge(out_stored, 16 * b)
                for t in range(TT // 2 * half, TT // 2 * (half + 1)):
                    last = nc.scalar.activation(res[:, t, :], psM[:, P * t:P * t + P], ACT.Identity,
                                                bias=small[:, 1, t:t + 1], scale=small[:, 0, t:t + 1])
                if half == 1:
                    last.then_inc(res_ready, 1)

            def silu(b, par, ch):
                n, k = NC1 * b + ch, nth(par, ch)
                act.wait_ge(h1_ready, n + 1)
                if from_chunk(n, 2):
                    act.wait_ge(a_ready, n - 1)
                nc.scalar.activation(s[k % 2][:, :], psH1[k % 2][:, :], ACT.Silu).then_inc(silu_ready, 1)

            def high_a(b, par, ch):
                n, k = NC1 * b + ch, nth(par, ch)
                act.wait_ge(a_ready, n + 1)
                if from_chunk(n, PART_BUFS):
                    act.wait_ge(y_added, n - PART_BUFS + 1)
                nc.scalar.copy(ah[k % PART_BUFS][:, :], a[k % A_BUFS][:, :]).then_inc(ah_ready, 1)

            def step(b, par):
                for ch in range(NC1):
                    silu(b, par, ch)
                    if ch:
                        high_a(b, par, ch - 1)
                    elif not first(b):
                        high_a(b - 1, 1 - par, NCH)
                    if ch in (1, 2) and from_chunk(b, 2):
                        normalise(b - 2, ch - 1)
                    if ch == 5 and follows(b, 1):
                        high_x(b + 1, 1 - par)
                    if ch == 8 and follows(b, 1):
                        copy_ct(b + 1, 1 - par)

            high_x(0, 0)
            copy_ct(0, 0)
            run_pairs(act, step)
            high_a(B - 1, 1, NCH)
            for b in (B - 2, B - 1):
                normalise(b, 0)
                normalise(b, 1)

        @block.tensor
        def _(pe):
            def turn_c(b, par):
                if not first(b):
                    pe.wait_ge(a_ready, NC1 * b - 2)
                wait_alone(pe, cparts_ready, b + 1)
                for t in range(TT):
                    last = nc.tensor.transpose(psC[1 - par][:, :].bitcast(BF16)[0:SPLIT * NEXP, P * t:P * t + P],
                                               cparts[:, t, :, :].rearrange("p s e -> p (s e)"), identb[:, :])
                last.then_inc(ct_transposed, 1)

            def turn_y(b):
                pe.wait_ge(yt_ready, b + 1)
                if not first(b):
                    pe.wait_ge(res_ready, b)
                for t in range(TT):
                    last = nc.tensor.transpose(psM[:, P * t:P * t + P], yt[:, P * t:P * t + P], identf[:, :])
                last.then_inc(y_turned, 1)

            def hidden(b, par, ch):
                n, k = NC1 * b + ch, nth(par, ch)
                at = slice(P * ch, P * ch + P)
                if from_chunk(n, 2):
                    pe.wait_ge(a_ready, n - 1)
                product(nc, psH1[k % 2][:, :], w["w1h"][:, at], w["w1l"][:, at], xh[par][:, :],
                        xl[par][:, :]).then_inc(h1_ready, 1)
                last = product(nc, psH3[k % 2][:, :], w["w3h"][:, at], w["w3l"][:, at], xh[par][:, :], xl[par][:, :])
                if ch == 0:
                    if first(b):
                        turn_c(0, 0)
                    pe.wait_ge(ct_copied, b + 1)
                if ch < NCH:
                    last = nc.tensor.matmul(psC[k % 2][:, :], w["selb"][:, ch, :], ct[par][:, :], start=True, stop=True)
                last.then_inc(hc_ready, 1)

            def down(b, par, ch):
                n, k = NC1 * b + ch, nth(par, ch)
                at = slice(P * ch, P * ch + P)
                pe.wait_ge(al_ready, n + 1)
                if ch == 0 and not first(b):
                    pe.wait_ge(yt_ready, b)
                product(nc, psY[:, :], w["w2h"][:, at], w["w2l"][:, at], ah[k % PART_BUFS][:, :], al[k % PART_BUFS][:, :],
                        start=(ch == 0), stop=(ch == NCH)).then_inc(y_added, 1)

            def step(b, par):
                pe.wait_ge(xl_ready, b + 1)
                for ch in range(NC1):
                    hidden(b, par, ch)
                    if ch == 3 and not first(b):
                        turn_y(b - 1)
                    if ch >= LAG:
                        down(b, par, ch - LAG)
                    elif not first(b):
                        down(b - 1, 1 - par, NC1 - LAG + ch)
                    if ch == 7 and follows(b, 1):
                        turn_c(b + 1, 1 - par)

            run_pairs(pe, step)
            for ch in range(NC1 - LAG, NC1):
                down(B - 1, 1, ch)
            turn_y(B - 1)

        @block.vector
        def _(dve):
            router, norm = Chain(dve, router_own), Chain(dve, norm_own)
            router.per = ROUTER_START + (ROUTER_GROUPS - 1) + (ROUTER_EXPERTS - 1)
            norm.per = 2 * TT + 4 + 3 * NEWTON

            def bcast(ap, shape):
                return ap.broadcast_to(shape)

            def comes_before(diff, before, result, less, n, part):
                if part == 0:
                    return nc.vector.scalar_tensor_tensor(
                        out=before[:, :, :, :], in0=diff[:, :, :, :], scalar=0.0,
                        in1=bcast(less.rearrange("p (a e) f -> p a e f", a=1), [P, TT, n, n]), op0=ALU.is_equal, op1=ALU.mult)
                if part == 1:
                    return nc.vector.scalar_tensor_tensor(
                        out=before[:, :, :, :], in0=diff[:, :, :, :], scalar=0.0, in1=before[:, :, :, :],
                        op0=ALU.is_gt, op1=ALU.add)
                return nc.vector.tensor_reduce(result[:, :, :], before[:, :, :, :], AX_X, ALU.add)

            def router_start(b, par, n):
                router.wait()
                if n == 0:
                    dve.wait_ge(ez_loaded, 16 * (b + 1))
                    router(nc.vector.tensor_reduce(esum[:, :], ez[:, :, :], AX_X, ALU.add))
                elif n == 1:
                    router(nc.vector.reciprocal(erec[:, :], esum[:, :]))
                elif n == 2:
                    router(nc.vector.tensor_tensor(scores[par][:, :, :], ez[:, :, :],
                                                   bcast(erec[:, :].rearrange("p (t a) -> p t a", a=1), [P, TT, NEXP]),
                                                   ALU.mult))
                else:
                    router(nc.vector.tensor_reduce(gmax[:, :, :].rearrange("p t g -> p (t g)"),
                                                   scores[par][:, :, :].rearrange("p t (g e) -> p (t g) e", g=NGRP),
                                                   AX_X, ALU.max))

            def router_groups(b, par, n):
                router.wait()
                if n == 0:
                    router(nc.vector.tensor_tensor(
                        gd[:, :, :, :], bcast(gmax[:, :, :].rearrange("p t (a f) -> p t a f", a=1), [P, TT, NGRP, NGRP]),
                        bcast(gmax[:, :, :].rearrange("p t (e a) -> p t e a", a=1), [P, TT, NGRP, NGRP]), ALU.subtract))
                elif n < 4:
                    router(comes_before(gd, ge, grank, less4, NGRP, n - 1))
                else:
                    nc.vector.scalar_tensor_tensor(
                        out=masked[:, :, :].rearrange("p t (g e) -> p (t g) e", g=NGRP),
                        in0=bcast(grank[:, :, :].rearrange("p t (g a) -> p (t g) a", a=1), [P, TT * NGRP, EPG]),
                        scalar=TOP_GROUPS - 0.5, in1=scores[par][:, :, :].rearrange("p t (g e) -> p (t g) e", g=NGRP),
                        op0=ALU.is_lt, op1=ALU.mult).then_inc(masked_ready, 1)

            def router_experts(b, par, n):
                router.wait()
                if n < 3:
                    if n == 0:
                        dve.wait_ge(ed_ready, b + 1)
                    router(comes_before(ed, ee, erank, less16, NEXP, n))
                elif n == 3:
                    router(nc.vector.scalar_tensor_tensor(out=c[:, :, :], in0=erank[:, :, :], scalar=TOP_EXPERTS - 0.5,
                                                          in1=scores[par][:, :, :], op0=ALU.is_lt, op1=ALU.mult))
                elif n == 4:
                    if not first(b):
                        dve.wait_ge(ct_transposed, b)
                    router(nc.vector.tensor_copy(cparts[:, :, 0, :], c[:, :, :]))
                elif n == 5:
                    router(nc.vector.tensor_tensor(crest[:, :, :], c[:, :, :], cparts[:, :, 0, :], ALU.subtract))
                elif n == 6:
                    router(nc.vector.tensor_copy(cparts[:, :, 1, :], crest[:, :, :]))
                else:
                    nc.vector.tensor_tensor(cparts[:, :, 2, :], crest[:, :, :], cparts[:, :, 1, :],
                                            ALU.subtract).then_inc(cparts_ready, 1)

            def norm_step(b, par, n):
                var, half, y, t = (small[:, m, :] for m in (2, 3, 0, 1))
                if n == 0:
                    dve.wait_ge(y_added, NC1 * b + NC1)
                    nc.vector.tensor_tensor(yt[:, :], psY[:, :], x1t[par][:, :], ALU.add).then_inc(yt_ready, 1)
                elif n == 1:
                    dve.wait_ge(y_turned, b + 1)
                    for m in range(TT):
                        norm(nc.vector.bn_stats(st[:, m, :], psM[:, P * m:P * m + P]))
                elif n == 2:
                    norm.wait(alone=True)
                    for m in range(TT):
                        norm(nc.vector.bn_aggr(mv[:, m, :], st[:, m, :]))
                elif n == 3:
                    norm.wait()
                    norm(nc.vector.tensor_scalar(var, mv[:, :, 1], EPS, None, ALU.add))
                elif n == 4:
                    norm.wait()
                    norm(nc.vector.tensor_scalar(t.bitcast(I32), var.bitcast(I32), 1, None, ALU.logical_shift_right))
                    norm(nc.vector.tensor_scalar(half, var, -0.5, None, ALU.mult))
                elif n == 5:
                    norm.wait()
                    norm(nc.vector.tensor_scalar(y.bitcast(I32), t.bitcast(I32), -1.0, float(0x5F3759DF),
                                                 ALU.mult, ALU.add))
                elif n == NORM_STEPS - 1:
                    norm.wait()
                    nc.vector.scalar_tensor_tensor(out=t, in0=mv[:, :, 0], scalar=-1.0, in1=y,
                                                   op0=ALU.mult, op1=ALU.mult).then_inc(scales_ready, 1)
                elif n % 3 == 0:
                    norm.wait()
                    norm(nc.vector.tensor_tensor(t, y, y, ALU.mult))
                elif n % 3 == 1:
                    norm.wait()
                    norm(nc.vector.tensor_tensor(t, t, half, ALU.mult))
                else:
                    norm.wait()
                    norm(nc.vector.scalar_tensor_tensor(out=y, in0=t, scalar=1.5, in1=y, op0=ALU.add, op1=ALU.mult))

            NORM_STEPS = 6 + 3 * NEWTON + 1
            NORM_BEFORE = {4: 0, 7: 1, 8: 2, 9: 3, 10: 4, 11: 5, 12: 6, 13: 8, 14: 10, 15: 12, 16: 14}
            NORM_BEHIND = {12: 7, 13: 9, 14: 11, 15: 13, 16: 15}
            EXPERT_SLOTS = {1: 0, 3: 1, 5: 2, 7: 3, 8: 4, 9: 5, 10: 6, 11: 7}
            START_AT, GROUPS_AT = 7, 11

            def between(b, par, slot):
                if not first(b) and slot in NORM_BEFORE:
                    norm_step(b - 1, 1 - par, NORM_BEFORE[slot])
                if follows(b, 1) and slot in EXPERT_SLOTS:
                    router_experts(b + 1, 1 - par, EXPERT_SLOTS[slot])
                if follows(b, 2) and START_AT <= slot < GROUPS_AT:
                    router_start(b + 2, par, slot - START_AT)
                if follows(b, 2) and GROUPS_AT <= slot < GROUPS_AT + ROUTER_GROUPS:
                    router_groups(b + 2, par, slot - GROUPS_AT)
                if not first(b) and slot in NORM_BEHIND:
                    norm_step(b - 1, 1 - par, NORM_BEHIND[slot])

            def step(b, par):
                for ch in range(NC1):
                    n, k = NC1 * b + ch, nth(par, ch)
                    dve.wait_ge(silu_ready, n + 1)
                    dve.wait_ge(hc_ready, n + 1)
                    if ch < NCH:
                        nc.vector.tensor_tensor(sh[k % 2][:, :], s[k % 2][:, :], psH3[k % 2][:, :],
                                                ALU.mult).then_inc(sh_ready, 1)
                    between(b, par, 2 * ch)
                    if from_chunk(n, A_BUFS):
                        dve.wait_ge(al_ready, n - A_BUFS + 1)
                    if ch < NCH:
                        dve.wait_ge(sh_ready, NCH * b + ch + 1)
                        last = nc.vector.tensor_tensor(a[k % A_BUFS][:, :], sh[k % 2][:, :], psC[k % 2][:, :], ALU.mult)
                    else:
                        last = nc.vector.tensor_tensor(a[k % A_BUFS][:, :], s[k % 2][:, :], psH3[k % 2][:, :], ALU.mult)
                    last.then_inc(a_ready, 1)
                    between(b, par, 2 * ch + 1)

            for n in range(ROUTER_START):
                router_start(0, 0, n)
            for n in range(ROUTER_GROUPS):
                router_groups(0, 0, n)
            for n in range(ROUTER_EXPERTS):
                router_experts(0, 0, n)
            for n in range(ROUTER_START):
                router_start(1, 1, n)
            for n in range(ROUTER_GROUPS):
                router_groups(1, 1, n)
            run_pairs(dve, step, router, norm)
            for n in range(NORM_STEPS):
                norm_step(B - 1, 1, n)


_INS = ["L0_attn_x", "L0_attn_Wqkv", "L0_attn_bqkv", "L0_attn_Wproj", "L0_attn_bproj", "L0_ffn_gate_w",
        "L0_ffn_w1", "L0_ffn_w2", "L0_ffn_w3", "L0_ffn_ws1", "L0_ffn_ws2", "L0_ffn_ws3"]
_OUTS = [((B, T, E), "float32")]


def kernel(**inputs):
    import concourse.bacc as _bacc
    from concourse.bass_utils import run_bass_kernel_spmd as _run

    nc = _bacc.Bacc("TRN2", target_bir_lowering=False, num_devices=1)
    arrays, args = {}, []
    for name in _INS:
        arrays[f"in_{name}"] = np.ascontiguousarray(inputs[name])
    arrays["in_constants"] = constants()
    for name, a in arrays.items():
        args.append(nc.dram_tensor(name, a.shape, mybir.dt.from_np(a.dtype), kind="ExternalInput").ap())
    for i, (shape, dtype) in enumerate(_OUTS):
        args.append(nc.dram_tensor(f"out_{i}", shape, mybir.dt.from_np(np.dtype(dtype)), kind="ExternalOutput").ap())
    layer_kernel(nc, *args)
    r = _run(nc, [arrays], core_ids=[0])
    return r.results[0]["out_0"]
```
